# Optimizing a Trainium2 kernel written in Bass

```python
import numpy as np
import jax
import jax.numpy as jnp

def _softmax(x, axis=-1):
    return jax.nn.softmax(x, axis=axis)

def _gelu(x):
    return jax.nn.gelu(x, approximate=True)

def _silu(x):
    return jax.nn.silu(x)

def _sigmoid(x):
    return jax.nn.sigmoid(x)

def _layernorm(x, axis=-1, eps=1e-05):
    m = jnp.mean(x, axis=axis, keepdims=True)
    v = jnp.var(x, axis=axis, keepdims=True)
    return (x - m) / jnp.sqrt(v + eps)

def _scatter_add(tgt, idx, src, axis=0):
    return tgt.at[idx].add(src)

def _segment_sum(src, seg, n):
    return jax.ops.segment_sum(src, seg, n)
kernel_name = 'mk_decoder_postln_d1_seqx_r4_881427'

def setup_inputs(seed: int=0):
    np.random.seed(seed)
    _w = jnp.asarray

    def _rec_inputs():
        import jax
        import jax.numpy as jnp
        _rk = jax.random.key(seed)
        x = -0.0005207 + 1.001 * jax.random.normal(jax.random.fold_in(_rk, 1), (16, 128, 256), jnp.float32)
        _lenS = 128 - jax.random.randint(jax.random.fold_in(_rk, 7), (16,), 0, max(1, 128 // 4) + 1, jnp.int32)
        _lenS2 = 128 - jax.random.randint(jax.random.fold_in(_rk, 8), (16,), 0, max(1, 128 // 4) + 1, jnp.int32)
        _ctx_1024P = jax.random.normal(jax.random.fold_in(_rk, 11), (16, 16, 256), jnp.float32)
        _ctx_1024c = jax.random.dirichlet(jax.random.fold_in(_rk, 511), 0.3 * jnp.ones((16,), jnp.float32), (16, 128))
        _ctx_1024t = jnp.einsum('bsk,bkd->bsd', _ctx_1024c, _ctx_1024P)
        _ctx_1024t = _ctx_1024t * jax.lax.rsqrt(jnp.mean(jnp.square(_ctx_1024t)) + 1e-12) * 0.953939
        ctx_1024 = -5.72187e-05 + 0.999849 * (_ctx_1024t + 0.3 * jax.random.normal(jax.random.fold_in(_rk, 611), (16, 128, 256), jnp.float32))
        return (x, ctx_1024)
    x, ctx_1024 = _rec_inputs()

    def _L0_attn_setup():
        import jax, jax.numpy as jnp
        import numpy as np
        import math
        N_HEADS, D_HEAD, D_MODEL = (16, 64, 256)
        B, S = (4, 512)
        NEG_MASK = -100000.0
        key = jax.random.key(seed)
        ks = jax.random.split(key, 9)
        bound = math.sqrt(6.0 / (D_MODEL + D_HEAD))

        def w(k):
            return jax.random.uniform(k, (N_HEADS, D_MODEL, D_HEAD), jnp.float32, -bound, bound)
        return {'x': jax.random.normal(ks[0], (B, S, D_MODEL), jnp.float32), 'Q_w': w(ks[1]), 'Q_b': jnp.zeros((N_HEADS, D_HEAD), jnp.float32), 'K_w': w(ks[2]), 'K_b': jnp.zeros((N_HEADS, D_HEAD), jnp.float32), 'V_w': w(ks[3]), 'V_b': jnp.zeros((N_HEADS, D_HEAD), jnp.float32), 'O_w': jax.random.uniform(ks[4], (N_HEADS, D_HEAD, D_MODEL), jnp.float32, -bound, bound), 'O_b': jnp.zeros((D_MODEL,), jnp.float32)}
    _L0_attn_all = _L0_attn_setup()
    _L0_attn_in = {k: v for k, v in _L0_attn_all.items() if k in ('Q_w', 'Q_b', 'K_w', 'K_b', 'V_w', 'V_b', 'O_w', 'O_b')}
    del _L0_attn_all

    def _L0_xattn_setup():
        import jax, jax.numpy as jnp
        import numpy as np
        key = jax.random.key(seed)
        ks = jax.random.split(key, 5)
        b, n_q, n_kv = (16, 128, 1024)
        query_dim, context_dim, heads, dim_head = (256, 256, 16, 64)
        inner = heads * dim_head
        x = jax.random.normal(ks[0], (b, n_q, query_dim), dtype=jnp.float32)
        context = jax.random.normal(ks[1], (b, n_kv, context_dim), dtype=jnp.float32)
        Wq = jax.random.normal(ks[2], (query_dim, inner), dtype=jnp.float32) * query_dim ** (-0.5)
        Wkv = jax.random.normal(ks[3], (context_dim, 2 * inner), dtype=jnp.float32) * context_dim ** (-0.5)
        Wout = jax.random.normal(ks[4], (inner, query_dim), dtype=jnp.float32) * inner ** (-0.5)
        bout = jnp.zeros((query_dim,), dtype=jnp.float32)
        return {'x': x, 'context': context, 'Wq': Wq, 'Wkv': Wkv, 'Wout': Wout, 'bout': bout}
    _L0_xattn_all = _L0_xattn_setup()
    _L0_xattn_in = {k: v for k, v in _L0_xattn_all.items() if k in ('Wq', 'Wkv', 'Wout', 'bout')}
    del _L0_xattn_all

    def _L0_ffn_setup():
        import jax, jax.numpy as jnp
        import numpy as np
        D_MODEL = 256
        HIDDEN = 256
        NUM_EXPERTS = 8
        TOP_K = 2
        key = jax.random.key(seed)
        ks = jax.random.split(key, 10)
        s = 0.02
        return {'x': jax.random.normal(ks[0], (2, 512, D_MODEL), dtype=jnp.float32), 'gate_w': jax.random.normal(ks[1], (NUM_EXPERTS, D_MODEL), dtype=jnp.float32) * s, 'up_w': jax.random.normal(ks[2], (NUM_EXPERTS, D_MODEL, HIDDEN), dtype=jnp.float32) * s, 'up_b': jnp.zeros((NUM_EXPERTS, HIDDEN), dtype=jnp.float32), 'down_w': jax.random.normal(ks[3], (NUM_EXPERTS, HIDDEN, D_MODEL), dtype=jnp.float32) * s, 'down_b': jnp.zeros((NUM_EXPERTS, D_MODEL), dtype=jnp.float32), 'sh_up_w': jax.random.normal(ks[4], (D_MODEL, HIDDEN), dtype=jnp.float32) * s, 'sh_up_b': jnp.zeros((HIDDEN,), dtype=jnp.float32), 'sh_down_w': jax.random.normal(ks[5], (HIDDEN, D_MODEL), dtype=jnp.float32) * s, 'sh_down_b': jnp.zeros((D_MODEL,), dtype=jnp.float32)}
    _L0_ffn_all = _L0_ffn_setup()
    _L0_ffn_in = {k: v for k, v in _L0_ffn_all.items() if k in ('gate_w', 'up_w', 'up_b', 'down_w', 'down_b', 'sh_up_w', 'sh_up_b', 'sh_down_w', 'sh_down_b')}
    del _L0_ffn_all
    return {'x': x, 'ctx_1024': ctx_1024, 'L0_attn_Q_w': _L0_attn_in['Q_w'], 'L0_attn_Q_b': _L0_attn_in['Q_b'], 'L0_attn_K_w': _L0_attn_in['K_w'], 'L0_attn_K_b': _L0_attn_in['K_b'], 'L0_attn_V_w': _L0_attn_in['V_w'], 'L0_attn_V_b': _L0_attn_in['V_b'], 'L0_attn_O_w': _L0_attn_in['O_w'], 'L0_attn_O_b': _L0_attn_in['O_b'], 'L0_xattn_Wq': _L0_xattn_in['Wq'], 'L0_xattn_Wkv': _L0_xattn_in['Wkv'], 'L0_xattn_Wout': _L0_xattn_in['Wout'], 'L0_xattn_bout': _L0_xattn_in['bout'], 'L0_ffn_gate_w': _L0_ffn_in['gate_w'], 'L0_ffn_up_w': _L0_ffn_in['up_w'], 'L0_ffn_up_b': _L0_ffn_in['up_b'], 'L0_ffn_down_w': _L0_ffn_in['down_w'], 'L0_ffn_down_b': _L0_ffn_in['down_b'], 'L0_ffn_sh_up_w': _L0_ffn_in['sh_up_w'], 'L0_ffn_sh_up_b': _L0_ffn_in['sh_up_b'], 'L0_ffn_sh_down_w': _L0_ffn_in['sh_down_w'], 'L0_ffn_sh_down_b': _L0_ffn_in['sh_down_b']}

def reference(x, ctx_1024, L0_attn_Q_w, L0_attn_Q_b, L0_attn_K_w, L0_attn_K_b, L0_attn_V_w, L0_attn_V_b, L0_attn_O_w, L0_attn_O_b, L0_xattn_Wq, L0_xattn_Wkv, L0_xattn_Wout, L0_xattn_bout, L0_ffn_gate_w, L0_ffn_up_w, L0_ffn_up_b, L0_ffn_down_w, L0_ffn_down_b, L0_ffn_sh_up_w, L0_ffn_sh_up_b, L0_ffn_sh_down_w, L0_ffn_sh_down_b):
    import jax
    import jax.numpy as jnp

    def _L0_attn_ref(x, Q_w, Q_b, K_w, K_b, V_w, V_b, O_w, O_b):
        import jax, jax.numpy as jnp
        import numpy as np
        import math
        N_HEADS, D_HEAD, D_MODEL = (16, 64, 256)
        B, S = (4, 512)
        NEG_MASK = -100000.0
        q = jnp.einsum('bpm,hmd->bphd', x, Q_w) + Q_b
        k = jnp.einsum('bpm,hmd->bphd', x, K_w) + K_b
        v = jnp.einsum('bpm,hmd->bphd', x, V_w) + V_b
        logits = jnp.einsum('bqhd,bkhd->bhqk', q, k) / math.sqrt(D_HEAD)
        s = logits.shape[-1]
        causal = jnp.triu(jnp.ones((s, s), dtype=bool), k=1)
        logits = jnp.where(causal, NEG_MASK, logits)
        scores = jax.nn.softmax(logits, axis=-1)
        attn = jnp.einsum('bhqk,bkhd->bqhd', scores, v)
        return jnp.einsum('bqhd,hdm->bqm', attn, O_w) + O_b

    def _L0_xattn_ref(x, context, Wq, Wkv, Wout, bout):
        import jax, jax.numpy as jnp
        import numpy as np
        heads, dim_head = (16, 64)
        b, n_q, _ = x.shape
        n_kv = context.shape[1]
        scale = dim_head ** (-0.5)
        q = x @ Wq
        kv = context @ Wkv
        k, v = jnp.split(kv, 2, axis=-1)

        def split_heads(t):
            bb, n, _ = t.shape
            return t.reshape(bb, n, heads, dim_head).transpose(0, 2, 1, 3)
        q, k, v = map(split_heads, (q, k, v))
        i_idx = jnp.arange(n_q)[:, None]
        j_idx = jnp.arange(n_kv)[None, :]
        mask = j_idx % n_q == i_idx
        sim = jnp.einsum('bhid,bhjd->bhij', q, k) * scale
        max_neg = -jnp.finfo(sim.dtype).max
        sim = jnp.where(mask[None, None, :, :], sim, max_neg)
        attn = jax.nn.softmax(sim, axis=-1)
        out = jnp.einsum('bhij,bhjd->bhid', attn, v)
        out = out.transpose(0, 2, 1, 3).reshape(b, n_q, heads * dim_head)
        return out @ Wout + bout

    def _L0_ffn_ref(x, gate_w, up_w, up_b, down_w, down_b, sh_up_w, sh_up_b, sh_down_w, sh_down_b):
        import jax, jax.numpy as jnp
        import numpy as np
        D_MODEL = 256
        HIDDEN = 256
        NUM_EXPERTS = 8
        TOP_K = 2
        b, s, d = x.shape
        xf = x.reshape(-1, d)
        shared = jax.nn.silu(x @ sh_up_w + sh_up_b) @ sh_down_w + sh_down_b
        logits = xf @ gate_w.T
        scores = jax.nn.softmax(logits, axis=-1)
        topk_w, topk_i = jax.lax.top_k(scores, TOP_K)
        topk_w = topk_w / (topk_w.sum(axis=-1, keepdims=True) + 1e-20)
        comb = (jax.nn.one_hot(topk_i, NUM_EXPERTS, dtype=xf.dtype) * topk_w[..., None]).sum(axis=1)
        h = jnp.einsum('nd,edh->neh', xf, up_w) + up_b
        h = jax.nn.silu(h)
        ye = jnp.einsum('neh,ehd->ned', h, down_w) + down_b
        y = jnp.einsum('ned,ne->nd', ye, comb).reshape(b, s, d)
        return y + shared
    x = _layernorm(x + _L0_attn_ref(x, L0_attn_Q_w, L0_attn_Q_b, L0_attn_K_w, L0_attn_K_b, L0_attn_V_w, L0_attn_V_b, L0_attn_O_w, L0_attn_O_b), axis=-1)
    x = _layernorm(x + _L0_xattn_ref(x, ctx_1024, L0_xattn_Wq, L0_xattn_Wkv, L0_xattn_Wout, L0_xattn_bout), axis=-1)
    x = _layernorm(x + _L0_ffn_ref(x, L0_ffn_gate_w, L0_ffn_up_w, L0_ffn_up_b, L0_ffn_down_w, L0_ffn_down_b, L0_ffn_sh_up_w, L0_ffn_sh_up_b, L0_ffn_sh_down_w, L0_ffn_sh_down_b), axis=-1)
    return x

_drawn_inputs = setup_inputs


def setup_inputs(seed=0):
    import zlib

    import numpy as np

    out = dict(_drawn_inputs(seed))
    spreads = {'L0_attn_Q_b': (0.0, 0.1),
     'L0_attn_K_b': (0.0, 0.8),
     'L0_attn_V_b': (0.0, 0.1),
     'L0_attn_O_b': (0.0, 0.1),
     'L0_xattn_bout': (0.0, 0.1),
     'L0_ffn_up_b': (0.0, 0.691),
     'L0_ffn_down_b': (0.0, 0.1),
     'L0_ffn_sh_up_b': (0.0, 0.477),
     'L0_ffn_sh_down_b': (0.0, 0.1)}
    factors = {}
    for name, (base, spread) in spreads.items():
        noise = np.random.default_rng([zlib.crc32(name.encode()), seed]).standard_normal(out[name].shape)
        drawn = base * np.exp(spread * noise) if base else spread * noise
        out[name] = jnp.asarray(drawn.astype(out[name].dtype))
    for name, factor in factors.items():
        out[name] = (out[name] * factor).astype(out[name].dtype)
    return out
```

```python
from contextlib import ExitStack

import concourse.bass as bass
from concourse import mybir

F32 = mybir.dt.float32
F32R = mybir.dt.float32r
U32 = mybir.dt.uint32
ALU = mybir.AluOpType
ACT = mybir.ActivationFunctionType
AX = mybir.AxisListType

P = 128
SEQS, S, D = 16, 128, 256
HEADS, DH = 16, 64
TOK = SEQS * S
KT = D // P
GROUP = 512
G = TOK // GROUP
GT = GROUP // P
QUADS = HEADS // 4
UNITS = QUADS * G
SLOTS = 2 * UNITS
SPQ = 2 * G
QW = 4 * DH
NX = 9
NE = 8
SCALE = DH ** -0.5
NEG = -1.0e30
EPS = 1e-5
INNER = HEADS * DH
IT = INNER // P

Q, K, V, O = range(4)
PARTS = (slice(Q, V), slice(V, O), slice(O, O + 1))
EPQ = NX // (QUADS - 1)
X2_TURN = 4
FRONT_STEPS = 27
BODY_STEPS = 23


def slices(i, n):
    return slice(i * n, (i + 1) * n)


def decoder_program(nc, x, ctx_in, w_quads, w_o, w_v, w_out, w_experts, w_gate, col_bias, row_bias,
                    down_bias, out):
    st = ExitStack()
    with st:
        def sb(name, shape, dt=F32):
            return st.enter_context(nc.sbuf_tensor(name, shape, dt))

        def sem(name):
            return st.enter_context(nc.semaphore(name))

        xt_hi = sb("xt_hi", [P, KT, TOK], F32R)
        xt_lo = sb("xt_lo", [P, KT, TOK], F32R)
        xacc = sb("xacc", [P, TOK // P, D])
        w_raw = sb("w_raw", [P, 4, KT, QW])
        w_hi = sb("w_hi", [P, 4, KT, QW], F32R)
        w_lo = sb("w_lo", [P, 4, KT, QW], F32R)
        qkv = sb("qkv", [P, 12 * GROUP])
        probs = sb("probs", [P, 2, 2, GROUP])
        probs_t = sb("probs_t", [P, 2, GROUP])
        ot_hi = sb("ot_hi", [P, 2, GROUP], F32R)
        ot_lo = sb("ot_lo", [P, 2, GROUP], F32R)
        up_hi = sb("up_hi", [P, NX, KT * D], F32R)
        up_lo = sb("up_lo", [P, NX, KT * D], F32R)
        down_hi = sb("down_hi", [P, NX, KT * D], F32R)
        down_lo = sb("down_lo", [P, NX, KT * D], F32R)
        ex_raw = sb("ex_raw", [P, 2, KT * D])
        wvo = sb("wvo", [P, KT, D])
        gate = sb("gate", [P, KT, NE])
        cols = sb("cols", [P, 2 * IT + IT + 2 * NX])
        rows = sb("rows", [1, 2 * D])
        brow = sb("brow", [1, 2 * D])
        bcast = sb("bcast", [P, 2 * D])
        down_b = sb("down_b", [NX, D])
        ident = sb("ident", [P, P])
        mask = sb("mask", [P, P])
        ones = sb("ones", [1, P])
        negmax = sb("negmax", [P, 2, 2, GT])
        sums = sb("sums", [P, 2, 2, GT])
        rsum = sb("rsum", [P, 2, GT])
        eps = sb("eps", [P, 1])
        iota8 = sb("iota8", [P, GT, NE])
        stats = sb("stats", [P, GT, 6])
        mv = sb("mv", [P, GT, 2])
        std = sb("std", [P, GT])
        rstd = sb("rstd", [P, GT])
        stats3 = sb("stats3", [P, GT, 6])
        mv3 = sb("mv3", [P, GT, 2])
        std3 = sb("std3", [P, GT])
        rstd3 = sb("rstd3", [P, GT])
        logits = sb("logits", [P, GT, NE])
        top8 = sb("top8", [P, GT, 8])
        idx8 = sb("idx8", [P, GT, 8], U32)
        idx2 = sb("idx2", [P, GT, 2])
        shifted = sb("shifted", [P, GT, NE + 2])
        expd = sb("expd", [P, GT, NE + 2])
        zsum = sb("zsum", [P, GT])
        rz = sb("rz", [P, GT])
        best = sb("best", [P, GT, 2])
        bsum = sb("bsum", [P, GT])
        rb = sb("rb", [P, GT])
        wbest = sb("wbest", [P, GT, 2])
        hot = sb("hot", [P, 2, GT, NE])
        comb = sb("comb", [P, GT, NX])
        comb_f = sb("comb_f", [P, GT, NX])
        comb_t = sb("comb_t", [NX, GROUP])

        qt = [qkv[:, (2 * b) * GROUP:(2 * b + 2) * GROUP].rearrange("p (a n) -> p a n", a=2) for b in range(2)]
        kt = [qkv[:, (4 + 2 * b) * GROUP:(6 + 2 * b) * GROUP].rearrange("p (a n) -> p a n", a=2) for b in range(2)]
        vv = [qkv[:, (8 + 2 * b) * GROUP:(10 + 2 * b) * GROUP].rearrange("p (t n) -> p t n", t=GT) for b in range(2)]
        wv_raw = qkv[:, 0:4 * GROUP].rearrange("p (k n) -> p k n", k=KT)
        wv_t = qkv[:, 4 * GROUP:8 * GROUP].rearrange("p (i n) -> p i n", i=IT)
        wout_raw = qkv[:, 8 * GROUP:12 * GROUP].rearrange("p (i n) -> p i n", i=IT)
        wo_all = probs[:, :, :, :].rearrange("p a b n -> p (a b n)").rearrange("p (i n) -> p i n", i=IT)
        def tile4(i):
            return qkv[:, 2 * i * GROUP:2 * (i + 1) * GROUP].rearrange("p (t n) -> p t n", t=GT)
        ctx_n, x1, x2, yacc = tile4(0), tile4(1), tile4(2), tile4(3)
        ctx_t = qkv[:, 8 * GROUP:10 * GROUP].rearrange("p (k n) -> p k n", k=KT)
        x2_t = qkv[:, 10 * GROUP:12 * GROUP].rearrange("p (k n) -> p k n", k=KT)
        hid = [probs[:, b, :, :] for b in range(2)]
        yout = probs_t[:, :, :].rearrange("p a n -> p (a n)").rearrange("p (t n) -> p t n", t=GT)
        hid_hi = [ot_hi[:, :, :], w_hi[:, 0:2, :, :].rearrange("p a k n -> p a (k n)")]
        hid_lo = [ot_lo[:, :, :], w_lo[:, 0:2, :, :].rearrange("p a k n -> p a (k n)")]

        bank = [st.enter_context(nc.psum_tensor(f"bank{i}", [P, GROUP], F32)) for i in range(8)]
        sc_bank = bank[0:2]
        tr_bank = bank[2:4]
        pv_bank = bank[4]
        pj_bank = bank[5:7]
        up_bank = [bank[0:2], bank[2:4]]
        dn_bank = bank[4:6]
        fr_bank = bank[6:8]

        in_x = [sem(f"in_x{b}") for b in range(G)]
        in_quad = sem("in_quad")
        in_wo, in_cols, in_cross, in_small = sem("in_wo"), sem("in_cols"), sem("in_cross"), sem("in_small")
        in_raw = [sem("in_raw_qk"), sem("in_raw_v"), sem("in_raw_o")]
        in_ex = [sem("in_up"), sem("in_down")]
        in_ctx, out_done = sem("in_ctx"), sem("out_done")
        consts_ready = sem("consts_ready")
        pool_step, pool_half = sem("pool_step"), sem("pool_half")
        xt_psum, xt_hi_ready, xt_ready = sem("xt_psum"), sem("xt_hi_ready"), sem("xt_ready")
        setup_pe, setup_act, setup_dve = sem("setup_pe"), sem("setup_act"), sem("setup_dve")
        w_split = [sem("w_split_qk"), sem("w_split_v"), sem("w_split_o")]
        ex_split = [sem("up_split"), sem("down_split")]
        proj_qk, proj_v, proj_o = sem("proj_qk"), sem("proj_v"), sem("proj_o")
        qk_ready, v_ready, o_added = sem("qk_ready"), sem("v_ready"), sem("o_added")
        scores, masked, exped = sem("scores"), sem("masked"), sem("exped")
        rsum_ready, probs_ready = sem("rsum_ready"), sem("probs_ready")
        transposed, pt_a, pt_b = sem("transposed"), sem("pt_a"), sem("pt_b")
        pv_done, ot_hi_ready, ot_ready = sem("pv_done"), sem("ot_hi_ready"), sem("ot_ready")
        var_ready, std_ready, dve_step = sem("var_ready"), sem("std_ready"), sem("dve_step")
        var3_ready, std3_ready = sem("var3_ready"), sem("std3_ready")
        ctx_tp, ctx_t_ready, cross_done, cross_used = (sem("ctx_tp"), sem("ctx_t_ready"), sem("cross_done"),
                                                       sem("cross_used"))
        x2_ready, x2_tp, x2_t_ready, x2_split = sem("x2_ready"), sem("x2_tp"), sem("x2_t_ready"), sem("x2_split")
        logit_done, shift_ready, exp_ready, comb_ready = (sem("logit_done"), sem("shift_ready"),
                                                          sem("exp_ready"), sem("comb_ready"))
        comb_tp, comb_t_ready = sem("comb_tp"), sem("comb_t_ready")
        bias_done, bias_used = sem("bias_done"), sem("bias_used")
        up_done, silu_done, hid_hi_done, hid_ready = sem("up_done"), sem("silu_done"), sem("hid_hi_done"), sem("hid_ready")
        down_done, down_used, y_ready = sem("down_done"), sem("down_used"), sem("y_ready")

        block = st.enter_context(nc.Block())

        def wait_apart(eng, semaphore, value, *more):
            pairs = [(semaphore, value), *zip(more[::2], more[1::2])]
            pairs = [(s, v if isinstance(v, int) else eng.to_reg(v)) for s, v in pairs]
            eng.wait_ge(consts_ready, 3)
            for s, v in pairs:
                eng.wait_ge(s, v)

        def three(pe, o, a_hi, a_lo, b_hi, b_lo, first, last):
            pe.matmul(o, a_hi, b_hi, start=first, stop=False)
            pe.matmul(o, a_hi, b_lo, start=False, stop=False)
            return pe.matmul(o, a_lo, b_hi, start=False, stop=last)

        class Slot:

            def __init__(s, t, pl):
                s.t, s.pl = t, pl
                s.static = t * SPQ + pl if isinstance(t, int) else None
                s.first = 0 if s.static is None else s.static
                s.par = pl % 2
                s.pp = pl % 2
                s.g = (pl // 2) % G
                s.ub = (pl // 2) % 2
                full = s.static is None
                p = s.static
                s.front = full or p < SLOTS
                s.back = full or 1 <= p <= SLOTS
                s.evac_o = full or 2 <= p <= SLOTS + 1
                s.proj = full or p // 2 + 1 < UNITS
                s.oproj = s.pp == 1 and (full or p >= 3)
                s.gn = (pl // 2 + 1) % G
                s.qn = t + (pl // 2 + 1) // G
                s.go = (pl // 2 - 1) % G
                s.qo = t + (pl // 2 - 1) // G

            def n(s, per_slot, c):
                return s.t * (SPQ * per_slot) + (s.pl * per_slot + c)

            def u(s, per_unit, c):
                return s.t * (G * per_unit) + (s.pl // 2 * per_unit + c)

        def all_slots(eng, emit):
            for p in range(3):
                emit(Slot(0, p))
            with eng.Fori(0, QUADS - 1) as t:
                for pl in range(3, 3 + SPQ):
                    emit(Slot(t, pl))
            for pl in range(3, SPQ + 2):
                emit(Slot(QUADS - 1, pl))

        @block.sync
        def _(sp):
            for b in range(G):
                sp.dma_start(xacc[:, slices(b, GT), :], x[slices(b, GROUP), :].rearrange("(t p) d -> p t d", p=P)
                             ).then_inc(in_x[b], 16)
                if b == 0:
                    sp.dma_start(w_raw[:, :, :, :], w_quads[0]).then_inc(in_quad, 16)
            with sp.Fori(1, QUADS) as t:
                for i, part in enumerate(PARTS):
                    sp.wait_ge(w_split[i], t)
                    src = w_quads[bass.ds(t, 1), :, part, :, :].rearrange("o p a k n -> (o p) a k n")
                    sp.dma_start(w_raw[:, part, :, :], src).then_inc(in_raw[i], 16)
                for e3 in range(EPQ):
                    e = t * EPQ + (e3 - EPQ)
                    for i in range(2):
                        src = w_experts[i, bass.ds(e, 1), :, :].rearrange("e p n -> (e p) n")
                        sp.dma_start(ex_raw[:, i, :], src).then_inc(in_ex[i], 16)
                    wait_apart(sp, ex_split[0], e + 1, ex_split[1], e + 1)
            def load_ctx(g):
                src = ctx_in[bass.ds(g * GROUP, GROUP), :].rearrange("(t p) d -> p t d", p=P)
                sp.dma_start(ctx_n, src).then_inc(in_ctx, 16)

            def store(g):
                sp.wait_ge(y_ready, g + 1)
                dst = out[bass.ds(g * GROUP, GROUP), :].rearrange("(t p) d -> p t d", p=P)
                sp.dma_start(dst, yout).then_inc(out_done, 16)

            sp.wait_ge(scores, 2 * SLOTS)
            load_ctx(0)
            with sp.Fori(0, G - 1) as g:
                sp.wait_ge(ctx_tp, g + 1)
                load_ctx(g + 1)
                store(g)
            store(G - 1)
            sp.wait_ge(out_done, 16 * G)

        @block.gpsimd
        def _(pool):
            nc.gpsimd.memset(ident[:, :], 0.0).then_inc(pool_step, 1)
            nc.gpsimd.memset(mask[:, :], 0.0).then_inc(pool_step, 1)
            pool.wait_ge(pool_step, 2)
            nc.gpsimd.affine_select(out=ident[:, :], in_=ident[:, :], compare_op=ALU.not_equal, fill=1.0, base=0,
                                    pattern=[[-1, P]], channel_multiplier=1).then_inc(consts_ready, 1)
            nc.gpsimd.affine_select(out=mask[:, :], in_=mask[:, :], compare_op=ALU.is_ge, fill=NEG, base=0,
                                    pattern=[[-1, P]], channel_multiplier=1).then_inc(consts_ready, 1)
            nc.gpsimd.iota(iota8[:, :, :], pattern=[[0, GT], [1, NE]], base=0, channel_multiplier=0,
                           allow_small_or_imprecise_dtypes=True).then_inc(consts_ready, 1)

            def split(hi, lo, raw, half, done):
                nc.gpsimd.tensor_copy(hi, raw).then_inc(half, 1)
                pool.wait_ge(half, done[1])
                nc.gpsimd.tensor_tensor(lo, raw, hi.bitcast(F32), ALU.subtract).then_inc(done[0], 1)

            steps_per_quad = len(PARTS) + 2 * EPQ
            with pool.Fori(1, QUADS) as t:
                for i, part in enumerate(PARTS):
                    wait_apart(pool, in_raw[i], t * 16, (proj_qk, proj_v, proj_o)[i], t * (G * (4, 2, 2)[i]))
                    split(w_hi[:, part, :, :], w_lo[:, part, :, :], w_raw[:, part, :, :], pool_half,
                          (w_split[i], t * steps_per_quad + (i + 1 - steps_per_quad)))
                for e3 in range(EPQ):
                    for i, (hi, lo) in enumerate(((up_hi, up_lo), (down_hi, down_lo))):
                        e = t * EPQ + (e3 - EPQ)
                        wait_apart(pool, in_ex[i], e * 16 + 16)
                        split(hi[:, bass.ds(e, 1), :].rearrange("p e n -> p (e n)"),
                              lo[:, bass.ds(e, 1), :].rearrange("p e n -> p (e n)"), ex_raw[:, i, :], pool_half,
                              (ex_split[i], t * steps_per_quad + (len(PARTS) + 2 * e3 + i + 1 - steps_per_quad)))

            with pool.Fori(0, G) as g:
                for e in range(NX):
                    pool.wait_ge(hid_hi_done, g * NX + (e + 1))
                    nc.gpsimd.tensor_tensor(hid_lo[e % 2], hid[e % 2], hid_hi[e % 2].bitcast(F32),
                                            ALU.subtract).then_inc(hid_ready, 1)

        @block.tensor
        def _(pe):
            pe.wait_ge(consts_ready, 1)
            for b in range(G):
                pe.wait_ge(in_x[b], 16)
                for k in range(KT):
                    for j in range(GT):
                        mm = pe.transpose(bank[b * KT + k][:, slices(j, P)], xacc[:, b * GT + j, slices(k, P)],
                                          ident[:, :])
                    mm.then_inc(xt_psum, 1)
            pe.wait_ge(in_cross, 32)
            for f in range(IT // 2):
                pe.wait_ge(xt_ready, f + 1)
                for i in range(2 * f, 2 * f + 2):
                    for k in range(KT):
                        mm = pe.transpose(bank[f][:, (i % 2) * D + k * P:(i % 2) * D + (k + 1) * P],
                                          wv_raw[:, k, slices(i, P)], ident[:, :])
                mm.then_inc(setup_pe, 1)
            pe.wait_ge(in_cols, 16)
            pe.wait_ge(in_wo, 16)
            pe.wait_ge(xt_ready, 5)
            for i in range(IT):
                mm = pe.matmul(bank[4][0:1, 0:D], cols[:, 2 * IT + i:2 * IT + i + 1], wo_all[:, i, :],
                               start=(i == 0), stop=(i == IT - 1))
            mm.then_inc(setup_pe, 1)
            pe.wait_ge(setup_act, IT // 2)
            pe.wait_ge(xt_ready, 7)
            for m in range(KT):
                for i in range(IT):
                    mm = pe.matmul(bank[6][:, slices(m, D)], wv_t[:, i, slices(m, P)], wout_raw[:, i, :],
                                   start=(i == 0), stop=(i == IT - 1))
            mm.then_inc(setup_pe, 1)
            pe.wait_ge(setup_dve, 2)
            pe.matmul(bank[5][:, :], ones[0:1, :], brow[0:1, :], start=True, stop=True).then_inc(setup_pe, 1)

            def project_qk(part, pair, g, o):
                for k in range(KT):
                    mm = three(pe, o, w_hi[:, part, k, slices(pair, P)], w_lo[:, part, k, slices(pair, P)],
                               xt_hi[:, k, slices(g, GROUP)], xt_lo[:, k, slices(g, GROUP)], k == 0, k == KT - 1)
                mm.then_inc(proj_qk, 1)

            def project_v(half, g, o):
                for j in range(2):
                    tok = slices(g * GT + half * 2 + j, P)
                    for k in range(KT):
                        mm = three(pe, o[:, slices(j, QW)], xt_hi[:, k, tok], xt_lo[:, k, tok],
                                   w_hi[:, V, k, :], w_lo[:, V, k, :], k == 0, k == KT - 1)
                mm.then_inc(proj_v, 1)

            def project_o(half, o):
                for j in range(2):
                    tok = slices(half * 2 + j, P)
                    for k in range(KT):
                        mm = three(pe, o[:, slices(j, D)], ot_hi[:, k, tok], ot_lo[:, k, tok],
                                   w_hi[:, O, k, :], w_lo[:, O, k, :], k == 0, k == KT - 1)
                mm.then_inc(proj_o, 1)

            pe.wait_ge(xt_ready, G * KT)
            pe.wait_ge(w_split[0], 1)
            for f in range(4):
                if f == 0:
                    pe.wait_ge(setup_dve, 3)
                elif f == 1:
                    pe.wait_ge(setup_act, IT // 2 + 1)
                else:
                    pe.wait_ge(qk_ready, f - 1)
                project_qk((Q, K)[f // 2], f % 2, 0, pj_bank[f % 2][:, :])
            for f in range(2):
                pe.wait_ge(qk_ready, 3 + f)
                pe.wait_ge(w_split[1], 1)
                project_v(f, 0, pj_bank[f][:, :])

            def slot(s):
                def fill(f):
                    o = pj_bank[f % 2][:, :]
                    if s.pp == 0 and s.proj:
                        if f < 2:
                            pe.wait_ge(v_ready, s.u(2, f + 1))
                            if s.static is None or s.static >= 4:
                                pe.wait_ge(o_added, s.u(2, f - 3))
                        else:
                            pe.wait_ge(qk_ready, s.u(4, 4 + f - 1))
                        if f == 0 and s.gn == 0:
                            pe.wait_ge(w_split[0], s.qn + 1)
                        project_qk((Q, K)[f // 2], f % 2, s.gn, o)
                    if s.pp == 1 and f < 2 and s.proj:
                        pe.wait_ge(qk_ready, s.u(4, 4 + 3 + f))
                        if f == 0 and s.gn == 0:
                            pe.wait_ge(w_split[1], s.qn + 1)
                        project_v(f, s.gn, o)
                    if s.oproj and f >= 2:
                        if s.proj:
                            pe.wait_ge(v_ready, s.u(2, 2 + f - 1))
                        else:
                            pe.wait_ge(o_added, s.u(2, f - 1 - 4))
                        if f == 2:
                            pe.wait_ge(ot_ready, s.u(2, 0))
                            if s.go == 0:
                                pe.wait_ge(w_split[2], s.qo + 1)
                        project_o(f - 2, o)

                def score(h):
                    if h == 0:
                        pe.wait_ge(qk_ready, s.u(4, 4))
                    if s.first > 0 or s.static is None:
                        pe.wait_ge(masked, s.n(8, -4 + 4 * h))
                    elif h == 0:
                        pe.wait_ge(setup_act, IT // 2)
                    for j in range(GT):
                        rows_h = slices(h, DH)
                        mm = pe.matmul(sc_bank[h][:, slices(j, P)], qt[s.ub][rows_h, s.pp, slices(j, P)],
                                       kt[s.ub][rows_h, s.pp, slices(j, P)], start=True, stop=True)
                    mm.then_inc(scores, 1)

                def turn(h):
                    pe.wait_ge(probs_ready, s.n(2, h - 1))
                    if s.static is None or s.static >= 2:
                        pe.wait_ge((pt_a, pt_b)[h], s.n(1, -1))
                    for j in range(GT):
                        mm = pe.transpose(tr_bank[h][:, slices(j, P)], probs[:, 1 - s.par, h, slices(j, P)], ident[:, :])
                    mm.then_inc(transposed, 1)

                if s.front:
                    score(0)
                fill(0)
                if s.back:
                    turn(0)
                if s.front:
                    score(1)
                fill(1)
                if s.back:
                    turn(1)
                fill(2)
                if s.back:
                    pe.wait_ge(pt_a, s.n(1, 0))
                    pe.wait_ge(pt_b, s.n(1, 0))
                    pe.wait_ge(v_ready, s.u(2, 2 if s.pp == 1 else 0))
                    if s.static is None or s.static >= 2:
                        pe.wait_ge(ot_ready, s.n(1, -1))
                    vb = vv[s.ub if s.pp == 1 else 1 - s.ub]
                    for j in range(GT):
                        for h in range(2):
                            c = (1 - s.pp) * P + h * DH
                            mm = pe.matmul(pv_bank[slices(h, DH), slices(j, P)], vb[:, j, c:c + DH],
                                           probs_t[:, h, slices(j, P)], start=True, stop=True)
                    mm.then_inc(pv_done, 1)
                fill(3)

            all_slots(pe, slot)

            def ctx_turn(g):
                pe.wait_ge(in_ctx, g * 16 + 16)
                if isinstance(g, int) and g == 0:
                    pe.wait_ge(o_added, 2 * UNITS)
                else:
                    pe.wait_ge(bias_used, g * 2)
                for k in range(KT):
                    for j in range(GT):
                        mm = pe.transpose(fr_bank[k][:, slices(j, P)], ctx_n[:, j, slices(k, P)], ident[:, :])
                mm.then_inc(ctx_tp, 1)

            def cross(g):
                pe.wait_ge(setup_act, IT // 2 + 1)
                pe.wait_ge(ctx_t_ready, g * 2 + 2)
                for j in range(GT):
                    for k in range(KT):
                        mm = pe.matmul(fr_bank[j // 2][:, slices(j % 2, D)], ctx_t[:, k, slices(j, P)], wvo[:, k, :],
                                       start=(k == 0), stop=(k == KT - 1))
                    if j % 2 == 1:
                        mm.then_inc(cross_done, 1)

            def x2_turn(g):
                pe.wait_ge(x2_ready, g + 1)
                for k in range(KT):
                    for j in range(GT):
                        mm = pe.transpose(fr_bank[k][:, slices(j, P)], x2[:, j, slices(k, P)], ident[:, :])
                mm.then_inc(x2_tp, 1)

            def route(g):
                pe.wait_ge(x2_t_ready, g * 2 + 2)
                for j in range(GT):
                    for k in range(KT):
                        mm = pe.matmul(fr_bank[0][:, slices(j, NE)], x2_t[:, k, slices(j, P)], gate[:, k, :],
                                       start=(k == 0), stop=(k == KT - 1))
                mm.then_inc(logit_done, 1)

            def comb_turn(g):
                pe.wait_ge(comb_ready, g + 1)
                for j in range(GT):
                    mm = pe.matmul(fr_bank[1][0:NX, slices(j, P)], comb[:, j, :], ident[:, :], start=True, stop=True)
                mm.then_inc(comb_tp, 1)

            def bias(g):
                pe.wait_ge(comb_t_ready, g + 1)
                for j in range(GT):
                    mm = pe.matmul(fr_bank[j // 2][:, slices(j % 2, D)], comb_t[:, slices(j, P)], down_b[:, :],
                                   start=True, stop=True)
                    if j % 2 == 1:
                        mm.then_inc(bias_done, 1)

            def up(g, e):
                if e == 0:
                    pe.wait_ge(x2_split, g + 1)
                if isinstance(g, int) and g == 0 and e < 2:
                    if e == 0:
                        pe.wait_ge(masked, 8 * SLOTS)
                        pe.wait_ge(pt_a, SLOTS)
                        pe.wait_ge(pt_b, SLOTS)
                        pe.wait_ge(ex_split[0], NX)
                        pe.wait_ge(ex_split[1], NX)
                else:
                    before = {0: 0, 1: -1}.get(e, e - 1)
                    pe.wait_ge(silu_done, g * (2 * NX) + 2 * before)
                for m in range(2):
                    for k in range(KT):
                        c = slice(k * D + m * P, k * D + (m + 1) * P)
                        cols_g = bass.ds(g * GROUP, GROUP)
                        mm = three(pe, up_bank[e % 2][m][:, :], up_hi[:, e, c], up_lo[:, e, c],
                                   xt_hi[:, k, cols_g], xt_lo[:, k, cols_g], k == 0, k == KT - 1)
                    mm.then_inc(up_done, 1)

            def down(g, e):
                pe.wait_ge(hid_ready, g * NX + (e + 1))
                for half in range(2):
                    if isinstance(g, int) and g == 0 and e == 0:
                        if half == 0:
                            pe.wait_ge(ot_ready, SLOTS)
                    else:
                        pe.wait_ge(down_used, g * (2 * NX) + (2 * e - 1 + half))
                    for j in (2 * half, 2 * half + 1):
                        for k in range(KT):
                            mm = three(pe, dn_bank[half][:, slices(j % 2, D)], hid_hi[e % 2][:, k, slices(j, P)],
                                       hid_lo[e % 2][:, k, slices(j, P)], down_hi[:, e, slices(k, D)],
                                       down_lo[:, e, slices(k, D)], k == 0, k == KT - 1)
                    mm.then_inc(down_done, 1)

            def ffn_and_front(g, front):
                bias(g)
                up(g, 0)
                for e in range(1, NX):
                    if front and e - 1 in front_pe:
                        front_pe[e - 1](g + 1)
                    up(g, e)
                    down(g, e - 1)
                down(g, NX - 1)

            front_pe = {0: ctx_turn, 1: cross, X2_TURN: x2_turn, X2_TURN + 1: route, X2_TURN + 3: comb_turn}
            for step in front_pe.values():
                step(0)
            ffn_and_front(0, True)
            with pe.Fori(1, G - 1) as g:
                ffn_and_front(g, True)
            ffn_and_front(G - 1, False)

        @block.scalar
        def _(act):
            act.dma_start(wo_all, w_o.rearrange("(i p) n -> p i n", p=P)).then_inc(in_wo, 16)
            act.dma_start(cols[:, :], col_bias).then_inc(in_cols, 16)
            act.dma_start(wv_raw, w_v.rearrange("(k p) n -> p k n", p=P)).then_inc(in_cross, 16)
            act.dma_start(wout_raw, w_out.rearrange("(i p) n -> p i n", p=P)).then_inc(in_cross, 16)
            act.dma_start(rows[:, :], row_bias).then_inc(in_small, 16)
            act.dma_start(down_b[:, :], down_bias).then_inc(in_small, 16)
            act.dma_start(gate[:, :, :], w_gate).then_inc(in_small, 16)
            for f in range(G * KT):
                act.wait_ge(xt_psum, f + 1)
                nc.scalar.activation(xt_hi[:, f % KT, slices(f // KT, GROUP)], bank[f][:, :], ACT.Copy
                                     ).then_inc(xt_hi_ready, 1)
            for f in range(IT // 2):
                act.wait_ge(setup_pe, f + 1)
                nc.scalar.activation(wv_t[:, 2 * f:2 * f + 2, :], bank[f][:, :].rearrange("p (i n) -> p i n", i=2),
                                     ACT.Copy).then_inc(setup_act, 1)
            act.wait_ge(setup_pe, IT // 2 + 2)
            nc.scalar.activation(wvo[:, :, :], bank[6][:, :].rearrange("p (k n) -> p k n", k=KT), ACT.Copy
                                 ).then_inc(setup_act, 1)

            def take_qk(f, g, quad, ub):
                dst = (qt, kt)[f // 2][ub][:, f % 2, :]
                b = cols[:, bass.ds(quad * 2 + ((f // 2) * IT + f % 2), 1)]
                nc.scalar.activation(dst, pj_bank[f % 2][:, :], ACT.Identity, bias=b).then_inc(qk_ready, 1)

            def take_v(f, ub):
                nc.scalar.activation(vv[ub][:, 2 * f:2 * f + 2, :],
                                     pj_bank[f][:, :].rearrange("p (j n) -> p j n", j=2), ACT.Copy).then_inc(v_ready, 1)

            act.wait_ge(in_cols, 16)
            for f in range(4):
                act.wait_ge(proj_qk, f + 1)
                take_qk(f, 0, 0, 0)
            for f in range(2):
                act.wait_ge(proj_v, f + 1)
                take_v(f, 0)

            def slot(s):
                def take(f):
                    if s.pp == 0 and s.proj:
                        wait_apart(act, proj_qk, s.u(4, 4 + f + 1))
                        take_qk(f, s.gn, s.qn, 1 - s.ub)
                    if s.pp == 1 and f < 2 and s.proj:
                        act.wait_ge(proj_v, s.u(2, 2 + f + 1))
                        take_v(f, 1 - s.ub)

                def exps(h):
                    for j in range(GT):
                        act.wait_ge(masked, s.n(8, 4 * h + j + 1))
                        tile = probs[:, s.par, h, slices(j, P)]
                        nc.scalar.activation(tile, tile, ACT.Exp, scale=-1.0, bias=negmax[:, s.par, h, j:j + 1],
                                             accum_out=sums[:, s.par, h, j:j + 1]).then_inc(exped, 1)

                if s.evac_o:
                    act.wait_ge(pv_done, s.n(1, -1))
                    if s.pp == 0 and (s.static is None or s.static >= 4):
                        act.wait_ge(proj_o, s.u(2, -2))
                    nc.scalar.activation(ot_hi[:, s.pp, :], pv_bank[:, :], ACT.Copy).then_inc(ot_hi_ready, 1)
                if s.front:
                    exps(0)
                take(0)
                if s.front:
                    exps(1)
                take(1)
                if s.back:
                    act.wait_ge(transposed, s.n(2, 0))
                    nc.scalar.activation(probs_t[:, 1, :], tr_bank[1][:, :], ACT.Copy).then_inc(pt_b, 1)
                take(2)
                take(3)

            all_slots(act, slot)

            def root1(g):
                act.wait_ge(var_ready, g * 2 + 1)
                nc.scalar.activation(std[:, :], mv[:, :, 1], ACT.Sqrt, bias=eps[:, 0:1]).then_inc(std_ready, 1)

            def root2(g):
                act.wait_ge(var_ready, g * 2 + 2)
                nc.scalar.activation(std[:, :], mv[:, :, 1], ACT.Sqrt, bias=eps[:, 0:1]).then_inc(std_ready, 1)

            def take_ctx(g):
                act.wait_ge(ctx_tp, g + 1)
                for k in range(KT):
                    nc.scalar.activation(ctx_t[:, k, :], fr_bank[k][:, :], ACT.Copy).then_inc(ctx_t_ready, 1)

            def take_x2(g):
                act.wait_ge(x2_tp, g + 1)
                for k in range(KT):
                    nc.scalar.activation(x2_t[:, k, :], fr_bank[k][:, :], ACT.Copy).then_inc(x2_t_ready, 1)

            def route_exp(g):
                act.wait_ge(shift_ready, g + 1)
                nc.scalar.activation(expd[:, :, :], shifted[:, :, :], ACT.Exp).then_inc(exp_ready, 1)

            def take_comb(g):
                act.wait_ge(comb_tp, g + 1)
                nc.scalar.activation(comb_t[:, :], fr_bank[1][0:NX, :], ACT.Copy).then_inc(comb_t_ready, 1)

            def hidden(g, e):
                if not (isinstance(g, int) and g == 0 and e < 2):
                    before = {0: 0, 1: -1}.get(e, e - 1)
                    act.wait_ge(hid_ready, g * NX + before)
                for m in range(2):
                    act.wait_ge(up_done, g * (2 * NX) + (2 * e + m + 1))
                    b = 3 * IT + 2 * e + m
                    nc.scalar.activation(hid[e % 2][:, m, :], up_bank[e % 2][m][:, :], ACT.Silu,
                                         bias=cols[:, b:b + 1]).then_inc(silu_done, 1)
                if not (isinstance(g, int) and g == 0 and e < 2):
                    act.wait_ge(down_done, g * (2 * NX) + 2 * before)
                act.wait_ge(silu_done, g * (2 * NX) + (2 * e + 2))
                nc.scalar.activation(hid_hi[e % 2], hid[e % 2], ACT.Copy).then_inc(hid_hi_done, 1)

            def ffn_and_front(g, front):
                for e in range(NX):
                    hidden(g, e)
                    if front:
                        for step in front_act.get(e, ()):
                            step(g + 1)
                act.wait_ge(var3_ready, g + 1)
                nc.scalar.activation(std3[:, :], mv3[:, :, 1], ACT.Sqrt, bias=eps[:, 0:1]).then_inc(std3_ready, 1)

            front_act = {0: (root1, take_ctx), 2: (root2,), X2_TURN: (take_x2,), X2_TURN + 1: (route_exp,),
                         X2_TURN + 3: (take_comb,)}
            for steps in front_act.values():
                for step in steps:
                    step(0)
            ffn_and_front(0, True)
            with act.Fori(1, G - 1) as g:
                ffn_and_front(g, True)
            ffn_and_front(G - 1, False)

        @block.vector
        def _(dve):
            nc.vector.memset(ones[:, :], 1.0).then_inc(dve_step, 1)
            nc.vector.memset(eps[:, :], EPS).then_inc(dve_step, 1)
            nc.vector.memset(comb[:, :, :], 1.0).then_inc(dve_step, 1)
            dve.wait_ge(in_quad, 16)
            for i, part in enumerate(PARTS):
                nc.vector.tensor_copy(w_hi[:, part, :, :], w_raw[:, part, :, :]).then_inc(dve_step, 1)
                dve.wait_ge(dve_step, 4 + i)
                nc.vector.tensor_tensor(w_lo[:, part, :, :], w_raw[:, part, :, :], w_hi[:, part, :, :].bitcast(F32),
                                        ALU.subtract).then_inc(w_split[i], 1)
            for f in range(G * KT):
                dve.wait_ge(xt_hi_ready, f + 1)
                hi = xt_hi[:, f % KT, slices(f // KT, GROUP)]
                nc.vector.tensor_tensor(xt_lo[:, f % KT, slices(f // KT, GROUP)], bank[f][:, :], hi.bitcast(F32),
                                        ALU.subtract).then_inc(xt_ready, 1)
            dve.wait_ge(in_small, 48)
            dve.wait_ge(setup_pe, IT // 2 + 1)
            nc.vector.tensor_tensor(brow[:, 0:D], bank[4][0:1, 0:D], rows[:, 0:D], ALU.add).then_inc(setup_dve, 1)
            nc.vector.tensor_copy(brow[:, D:2 * D], rows[:, D:2 * D]).then_inc(setup_dve, 1)
            dve.wait_ge(setup_pe, IT // 2 + 3)
            nc.vector.tensor_copy(bcast[:, :], bank[5][:, :]).then_inc(setup_dve, 1)
            dve.wait_ge(setup_dve, 3)
            nc.vector.tensor_tensor(xacc[:, :, :], xacc[:, :, :],
                                    bcast[:, 0:D].unsqueeze(1).to_broadcast([P, TOK // P, D]), ALU.add
                                    ).then_inc(setup_dve, 1)
            dve.wait_ge(consts_ready, 3)
            dve.wait_ge(setup_dve, 4)

            def slot(s):
                def mask_and_max(h):
                    wait_apart(dve, scores, s.n(2, h + 1))
                    for j in range(GT):
                        nc.vector.tensor_tensor_reduce(
                            probs[:, s.par, h, slices(j, P)], sc_bank[h][:, slices(j, P)], mask[:, :], -SCALE, 3.0e38,
                            ALU.add, ALU.min, negmax[:, s.par, h, j:j + 1]).then_inc(masked, 1)

                def normalise(h):
                    dve.wait_ge(exped, s.n(8, 4 * h + 4))
                    nc.vector.reciprocal(rsum[:, h, :], sums[:, s.par, h, :]).then_inc(rsum_ready, 1)
                    dve.wait_ge(rsum_ready, s.n(2, h + 1))
                    tile = probs[:, s.par, h, :].rearrange("p (j k) -> p j k", j=GT)
                    nc.vector.tensor_tensor(tile, tile, rsum[:, h, :].unsqueeze(2).to_broadcast([P, GT, P]), ALU.mult
                                            ).then_inc(probs_ready, 1)

                def add_o(half):
                    dve.wait_ge(proj_o, s.u(2, half - 1))
                    tile = xacc[:, s.go * GT + 2 * half:s.go * GT + 2 * half + 2, :]
                    nc.vector.tensor_tensor(tile, pj_bank[half][:, :].rearrange("p (j n) -> p j n", j=2), tile,
                                            ALU.add).then_inc(o_added, 1)

                if s.evac_o:
                    dve.wait_ge(ot_hi_ready, s.n(1, -1))
                    nc.vector.tensor_tensor(ot_lo[:, s.pp, :], pv_bank[:, :], ot_hi[:, s.pp, :].bitcast(F32),
                                            ALU.subtract).then_inc(ot_ready, 1)
                if s.front:
                    mask_and_max(0)
                if s.back:
                    dve.wait_ge(transposed, s.n(2, -1))
                    nc.vector.tensor_copy(probs_t[:, 0, :], tr_bank[0][:, :]).then_inc(pt_a, 1)
                if s.front:
                    normalise(0)
                    mask_and_max(1)
                if s.oproj:
                    add_o(0)
                if s.front:
                    normalise(1)
                if s.oproj:
                    add_o(1)

            all_slots(dve, slot)

            class Chain:
                per_body = BODY_STEPS
                c, g = 6, 0

                def step(s, ins, wait=lambda eng, semaphore, value: eng.wait_ge(semaphore, value)):
                    s.c += 1
                    ins.then_inc(dve_step, 1)
                    wait(dve, dve_step, s.g * s.per_body + s.c)

            ch = Chain()

            def statistics(src, st6, m, ready):
                for j in range(GT):
                    last = nc.vector.bn_stats(st6[:, j, :], src(j))
                ch.step(last, wait_apart)
                for j in range(GT):
                    last = nc.vector.bn_aggr(m[:, j, :], st6[:, j, :])
                last.then_inc(ready, 1)

            def apply(src, dst, m, root, r):
                ch.step(nc.vector.reciprocal(r[:, :], root[:, :]))
                for j in range(GT):
                    last = nc.vector.tensor_scalar(dst[:, j, :], src(j), m[:, j, 0:1], r[:, j:j + 1],
                                                   ALU.subtract, ALU.mult)
                return last

            def tile_of(g):
                def src(j):
                    return xacc[:, bass.ds(g * GT + j, 1), :].rearrange("p t n -> p (t n)")
                return src

            def norm1_stats(g):
                statistics(tile_of(g), stats, mv, var_ready)

            def norm1(g):
                dve.wait_ge(std_ready, g * 2 + 1)
                ch.step(apply(tile_of(g), x1, mv, std, rstd))
                ch.step(nc.vector.tensor_tensor(x1, x1, bcast[:, D:2 * D].unsqueeze(1).to_broadcast([P, GT, D]),
                                                ALU.add))

            def add_cross(g):
                for half in range(2):
                    dve.wait_ge(cross_done, g * 2 + (half + 1))
                    tile = x1[:, 2 * half:2 * half + 2, :]
                    last = nc.vector.tensor_tensor(tile, fr_bank[half][:, :].rearrange("p (j n) -> p j n", j=2), tile,
                                                   ALU.add)
                ch.step(last)
                statistics(lambda j: x1[:, j, :], stats, mv, var_ready)

            def norm2(g):
                dve.wait_ge(std_ready, g * 2 + 2)
                apply(lambda j: x1[:, j, :], x2, mv, std, rstd).then_inc(x2_ready, 1)

            def split_x2(g):
                dve.wait_ge(x2_t_ready, g * 2 + 2)
                cols_g = bass.ds(g * GROUP, GROUP)
                ch.step(nc.vector.tensor_copy(xt_hi[:, :, cols_g], x2_t))
                nc.vector.tensor_tensor(xt_lo[:, :, cols_g], x2_t, xt_hi[:, :, cols_g].bitcast(F32), ALU.subtract
                                        ).then_inc(x2_split, 1)

            def best_two(g):
                dve.wait_ge(logit_done, g + 1)
                ch.step(nc.vector.tensor_copy(logits[:, :, :],
                                              fr_bank[0][:, 0:GT * NE].rearrange("p (j e) -> p j e", j=GT)),
                        wait_apart)
                for j in range(GT):
                    last = nc.vector.max(top8[:, j, :], logits[:, j, :])
                ch.step(last)
                top = top8[:, :, 0:1]
                nc.vector.tensor_tensor(shifted[:, :, 0:NE], logits[:, :, :], top.to_broadcast([P, GT, NE]), ALU.subtract)
                nc.vector.tensor_tensor(shifted[:, :, NE:NE + 2], top8[:, :, 0:2], top.to_broadcast([P, GT, 2]),
                                        ALU.subtract).then_inc(shift_ready, 1)
                for j in range(GT):
                    last = nc.vector.max_index(idx8[:, j, :], top8[:, j, :], logits[:, j, :])
                ch.step(last)
                ch.step(nc.vector.tensor_copy(idx2[:, :, :], idx8[:, :, 0:2]))
                for i in range(2):
                    last = nc.vector.tensor_tensor(hot[:, i, :, :], iota8[:, :, :],
                                                   idx2[:, :, i:i + 1].to_broadcast([P, GT, NE]), ALU.is_equal)
                ch.step(last)

            def weigh(g):
                dve.wait_ge(exp_ready, g + 1)
                ch.step(nc.vector.tensor_reduce(zsum[:, :], expd[:, :, 0:NE], AX.X, ALU.add))
                ch.step(nc.vector.reciprocal(rz[:, :], zsum[:, :]))
                ch.step(nc.vector.tensor_tensor(best[:, :, :], expd[:, :, NE:NE + 2],
                                                rz[:, :].unsqueeze(2).to_broadcast([P, GT, 2]), ALU.mult))
                ch.step(nc.vector.tensor_reduce(bsum[:, :], best[:, :, :], AX.X, ALU.add))
                ch.step(nc.vector.tensor_scalar(bsum[:, :], bsum[:, :], 1e-20, None, ALU.add))
                ch.step(nc.vector.reciprocal(rb[:, :], bsum[:, :]))
                ch.step(nc.vector.tensor_tensor(wbest[:, :, :], best[:, :, :],
                                                rb[:, :].unsqueeze(2).to_broadcast([P, GT, 2]), ALU.mult))
                for i in range(2):
                    last = nc.vector.tensor_tensor(hot[:, i, :, :], hot[:, i, :, :],
                                                   wbest[:, :, i:i + 1].to_broadcast([P, GT, NE]), ALU.mult)
                ch.step(last)
                nc.vector.tensor_tensor(comb[:, :, 0:NE], hot[:, 0, :, :], hot[:, 1, :, :], ALU.add
                                        ).then_inc(comb_ready, 1)

            def start_y(g):
                dve.wait_ge(comb_ready, g + 1)
                nc.vector.tensor_copy(comb_f[:, :, :], comb[:, :, :])
                if not (isinstance(g, int) and g == 0):
                    dve.wait_ge(y_ready, g)
                for half in range(2):
                    dve.wait_ge(bias_done, g * 2 + (half + 1))
                    nc.vector.tensor_tensor(yacc[:, 2 * half:2 * half + 2, :],
                                            fr_bank[half][:, :].rearrange("p (j n) -> p j n", j=2),
                                            x2[:, 2 * half:2 * half + 2, :], ALU.add).then_inc(bias_used, 1)
                dve.wait_ge(bias_used, g * 2 + 2)

            def add_expert(g, e):
                for half in range(2):
                    dve.wait_ge(down_done, g * (2 * NX) + (2 * e + half + 1))
                    if e > 0:
                        dve.wait_ge(down_used, g * (2 * NX) + (2 * e - 1 + half))
                    for j in (2 * half, 2 * half + 1):
                        last = nc.vector.scalar_tensor_tensor(
                            out=yacc[:, j, :], in0=dn_bank[half][:, slices(j % 2, D)], scalar=comb_f[:, j, e:e + 1],
                            in1=yacc[:, j, :], op0=ALU.mult, op1=ALU.add)
                    last.then_inc(down_used, 1)

            def finish(g):
                dve.wait_ge(down_used, g * (2 * NX) + 2 * NX)
                statistics(lambda j: yacc[:, j, :], stats3, mv3, var3_ready)
                dve.wait_ge(std3_ready, g + 1)
                if not (isinstance(g, int) and g == 0):
                    dve.wait_ge(out_done, g * 16)
                apply(lambda j: yacc[:, j, :], yout, mv3, std3, rstd3).then_inc(y_ready, 1)

            def ffn_and_front(g, front):
                ch.g, ch.c = g, FRONT_STEPS
                start_y(g)
                for e in range(NX):
                    if front:
                        for step in front_dve.get(e, ()):
                            step(g + 1)
                    add_expert(g, e)
                finish(g)
                if front:
                    ch.per_body == ch.c - FRONT_STEPS or fail(ch.c - FRONT_STEPS)

            def fail(n):
                raise ValueError(f"{n} steps of VectorE per group")

            front_dve = {0: (norm1_stats, norm1), 1: (add_cross, norm2), X2_TURN + 1: (split_x2,),
                         X2_TURN + 2: (best_two,), X2_TURN + 3: (weigh,)}
            dve.wait_ge(o_added, 2 * UNITS)
            for steps in front_dve.values():
                for step in steps:
                    step(0)
            ch.c == FRONT_STEPS or fail(ch.c)
            ffn_and_front(0, True)
            with dve.Fori(1, G - 1) as g:
                ffn_and_front(g, True)
            ffn_and_front(G - 1, False)


def kernel(**inputs):
    import numpy as np
    import concourse.bacc as bacc
    from concourse.bass_utils import run_bass_kernel_spmd

    a = {k: np.asarray(v) for k, v in inputs.items()}

    def heads_in(w):
        return w.reshape(QUADS, 4, KT, P, DH).transpose(0, 3, 2, 1, 4).reshape(QUADS, P, KT, QW)

    w_o = a["L0_attn_O_w"].reshape(INNER, D)
    o_quads = w_o.reshape(QUADS, KT, P, D).transpose(0, 2, 1, 3)
    up = np.concatenate([a["L0_ffn_up_w"], a["L0_ffn_sh_up_w"][None]])
    down = np.concatenate([a["L0_ffn_down_w"], a["L0_ffn_sh_down_w"][None]])
    up_b = np.concatenate([a["L0_ffn_up_b"], a["L0_ffn_sh_up_b"][None]])

    def by_partition(w):
        return w.reshape(NX, KT, P, D).transpose(0, 2, 1, 3).reshape(NX, P, KT * D)

    arrays = {
        "x": a["x"].reshape(TOK, D),
        "ctx_in": a["ctx_1024"].reshape(TOK, D),
        "w_quads": np.stack([heads_in(a["L0_attn_Q_w"]), heads_in(a["L0_attn_K_w"]), heads_in(a["L0_attn_V_w"]),
                             o_quads], axis=2),
        "w_o": w_o,
        "w_v": a["L0_xattn_Wkv"][:, INNER:],
        "w_out": a["L0_xattn_Wout"],
        "w_experts": np.stack([by_partition(up), by_partition(down)]),
        "w_gate": a["L0_ffn_gate_w"].T.reshape(KT, P, NE).transpose(1, 0, 2),
        "col_bias": np.concatenate([a[f"L0_attn_{n}_b"].reshape(IT, P).T for n in "QKV"]
                                   + [up_b.reshape(2 * NX, P).T], axis=1),
        "row_bias": np.concatenate([a["L0_attn_O_b"], a["L0_xattn_bout"]])[None],
        "down_bias": np.concatenate([a["L0_ffn_down_b"], a["L0_ffn_sh_down_b"][None]]),
    }
    arrays = {k: np.ascontiguousarray(v) for k, v in arrays.items()}
    nc = bacc.Bacc("TRN2", target_bir_lowering=False, num_devices=1)
    aps = {k: nc.dram_tensor(f"in_{k}", v.shape, F32, kind="ExternalInput").ap() for k, v in arrays.items()}
    out = nc.dram_tensor("out_0", (TOK, D), F32, kind="ExternalOutput").ap()
    decoder_program(nc, out=out, **aps)
    r = run_bass_kernel_spmd(nc, [{f"in_{k}": v for k, v in arrays.items()}], core_ids=[0])
    return r.results[0]["out_0"].reshape(SEQS, S, D)
```

```python
from contextlib import ExitStack

import concourse.bass as bass
from concourse import mybir

F32 = mybir.dt.float32
F32R = mybir.dt.float32r
U32 = mybir.dt.uint32
ALU = mybir.AluOpType
ACT = mybir.ActivationFunctionType
AX = mybir.AxisListType

P = 128
SEQS, S, D = 16, 128, 256
HEADS, DH = 16, 64
TOK = SEQS * S
KT = D // P
GROUP = 512
G = TOK // GROUP
GT = GROUP // P
QUADS = HEADS // 4
UNITS = QUADS * G
SLOTS = 2 * UNITS
SPQ = 2 * G
QW = 4 * DH
NX = 9
NE = 8
SCALE = DH ** -0.5
NEG = -1.0e30
EPS = 1e-5
INNER = HEADS * DH
IT = INNER // P

Q, K, V, O = range(4)
PARTS = (slice(Q, V), slice(V, O), slice(O, O + 1))
EPQ = NX // (QUADS - 1)
LAG = 2
CROSS, X2_TURN, ROUTE = 2, 5, 6
FRONT_STEPS = 25
BODY_STEPS = 22


def slices(i, n):
    return slice(i * n, (i + 1) * n)


def decoder_program(nc, x, x_t, ctx_t_in, w_quads, w_cross, w_experts, w_gate, col_bias, row_bias, down_bias,
                    out):
    st = ExitStack()
    with st:
        def sb(name, shape, dt=F32):
            return st.enter_context(nc.sbuf_tensor(name, shape, dt))

        def sem(name):
            return st.enter_context(nc.semaphore(name))

        xt_hi = sb("xt_hi", [P, KT, TOK], F32R)
        xt_lo = sb("xt_lo", [P, KT, TOK], F32R)
        xacc = sb("xacc", [P, TOK // P, D])
        w_raw = sb("w_raw", [P, 4, KT, QW])
        w_hi = sb("w_hi", [P, 4, KT, QW], F32R)
        w_lo = sb("w_lo", [P, 4, KT, QW], F32R)
        qkv = sb("qkv", [P, 12 * GROUP])
        probs = sb("probs", [P, 2, 2, GROUP])
        probs_t = sb("probs_t", [P, 2, GROUP])
        ot_hi = sb("ot_hi", [P, 2, GROUP], F32R)
        ot_lo = sb("ot_lo", [P, 2, GROUP], F32R)
        up_hi = sb("up_hi", [P, NX, KT * D], F32R)
        up_lo = sb("up_lo", [P, NX, KT * D], F32R)
        down_hi = sb("down_hi", [P, NX, KT * D], F32R)
        down_lo = sb("down_lo", [P, NX, KT * D], F32R)
        ex_raw = sb("ex_raw", [P, 2, KT * D])
        wvo = sb("wvo", [P, KT, D])
        gate = sb("gate", [P, KT, NE])
        cols = sb("cols", [P, 2 * IT + IT + 2 * NX])
        bcast = sb("bcast", [P, 2 * D])
        down_b = sb("down_b", [NX, D])
        ident = sb("ident", [P, P])
        mask = sb("mask", [P, P])
        negmax = sb("negmax", [P, 2, 2, GT])
        sums = sb("sums", [P, 2, 2, GT])
        rsum = sb("rsum", [P, 2, GT])
        eps = sb("eps", [P, 1])
        iota8 = sb("iota8", [P, GT, NE])
        stats = sb("stats", [P, GT, 6])
        mv = sb("mv", [P, GT, 2])
        std = sb("std", [P, GT])
        rstd = sb("rstd", [P, GT])
        stats3 = sb("stats3", [P, GT, 6])
        mv3 = sb("mv3", [P, GT, 2])
        std3 = sb("std3", [P, GT])
        rstd3 = sb("rstd3", [P, GT])
        logits = sb("logits", [P, GT, NE])
        top8 = sb("top8", [P, GT, 8])
        idx8 = sb("idx8", [P, GT, 8], U32)
        idx2 = sb("idx2", [P, GT, 2])
        shifted = sb("shifted", [P, GT, NE + 2])
        expd = sb("expd", [P, GT, NE + 2])
        zsum = sb("zsum", [P, GT])
        rz = sb("rz", [P, GT])
        best = sb("best", [P, GT, 2])
        bsum = sb("bsum", [P, GT])
        rb = sb("rb", [P, GT])
        wbest = sb("wbest", [P, GT, 2])
        hot = sb("hot", [P, 2, GT, NE])
        comb = sb("comb", [P, GT, NX])
        comb_f = sb("comb_f", [P, GT, NX])
        comb_t = sb("comb_t", [NX, GROUP])

        qt = [qkv[:, (2 * b) * GROUP:(2 * b + 2) * GROUP].rearrange("p (a n) -> p a n", a=2) for b in range(2)]
        kt = [qkv[:, (4 + 2 * b) * GROUP:(6 + 2 * b) * GROUP].rearrange("p (a n) -> p a n", a=2) for b in range(2)]
        vv = [qkv[:, (8 + 2 * b) * GROUP:(10 + 2 * b) * GROUP].rearrange("p (t n) -> p t n", t=GT) for b in range(2)]
        xt_raw = [xacc[:, slices(b, GT), :].rearrange("p t n -> p (t n)").rearrange("p (k n) -> p k n", k=KT)
                  for b in range(G)]
        w_flat = w_raw[:, :, :, :].rearrange("p a k n -> p (a k n)")
        x1 = w_flat[:, 0:2 * GROUP].rearrange("p (t n) -> p t n", t=GT)
        ctx_t = w_flat[:, 2 * GROUP:4 * GROUP].rearrange("p (k n) -> p k n", k=KT)
        x2 = qkv[:, 0:2 * GROUP].rearrange("p (t n) -> p t n", t=GT)
        x2_t = qkv[:, 4 * GROUP:6 * GROUP].rearrange("p (k n) -> p k n", k=KT)
        yacc = qkv[:, 2 * GROUP:4 * GROUP].rearrange("p (t n) -> p t n", t=GT)
        hid = [probs[:, b, :, :] for b in range(2)]
        yout = probs_t[:, :, :].rearrange("p a n -> p (a n)").rearrange("p (t n) -> p t n", t=GT)
        hid_hi = [ot_hi[:, :, :], w_hi[:, 0:2, :, :].rearrange("p a k n -> p a (k n)")]
        hid_lo = [ot_lo[:, :, :], w_lo[:, 0:2, :, :].rearrange("p a k n -> p a (k n)")]

        bank = [st.enter_context(nc.psum_tensor(f"bank{i}", [P, GROUP], F32)) for i in range(8)]
        sc_bank = bank[0:2]
        tr_bank = bank[2:4]
        pv_bank = bank[4]
        pj_bank = bank[5:7]
        up_bank = [bank[0:2], bank[2:4]]
        dn_bank = bank[4:6]
        fr_bank = bank[6:8]

        in_xt = [sem(f"in_xt{b}") for b in range(G)]
        in_x = [sem(f"in_x{b}") for b in range(G)]
        in_quad = [sem("in_quad_qk"), sem("in_quad_v"), sem("in_quad_o")]
        in_cols, in_bcast, in_small, in_cross = sem("in_cols"), sem("in_bcast"), sem("in_small"), sem("in_cross")
        in_raw = [sem("in_raw_qk"), sem("in_raw_v"), sem("in_raw_o")]
        in_ex = [sem("in_up"), sem("in_down")]
        in_ctx, out_done = sem("in_ctx"), sem("out_done")
        consts_ready = sem("consts_ready")
        pool_step, pool_half = sem("pool_step"), sem("pool_half")
        xt_hi_ready, xt_ready, x_ready = sem("xt_hi_ready"), sem("xt_ready"), sem("x_ready")
        wvo_step, wvo_ready = sem("wvo_step"), sem("wvo_ready")
        w_split = [sem("w_split_qk"), sem("w_split_v"), sem("w_split_o")]
        ex_split = [sem("up_split"), sem("down_split")]
        proj_qk, proj_v, proj_o = sem("proj_qk"), sem("proj_v"), sem("proj_o")
        qk_ready, v_ready, o_added = sem("qk_ready"), sem("v_ready"), sem("o_added")
        scores, masked, exped = sem("scores"), sem("masked"), sem("exped")
        rsum_ready, probs_ready = sem("rsum_ready"), sem("probs_ready")
        transposed, pt_a, pt_b = sem("transposed"), sem("pt_a"), sem("pt_b")
        pv_done, ot_hi_ready, ot_ready = sem("pv_done"), sem("ot_hi_ready"), sem("ot_ready")
        var_ready, std_ready, dve_step = sem("var_ready"), sem("std_ready"), sem("dve_step")
        var3_ready, std3_ready = sem("var3_ready"), sem("std3_ready")
        cross_done, cross_used = sem("cross_done"), sem("cross_used")
        x2_ready, x2_tp, x2_t_ready, x2_split = sem("x2_ready"), sem("x2_tp"), sem("x2_t_ready"), sem("x2_split")
        logit_done, shift_ready, exp_ready, comb_ready = (sem("logit_done"), sem("shift_ready"),
                                                          sem("exp_ready"), sem("comb_ready"))
        comb_tp, comb_t_ready = sem("comb_tp"), sem("comb_t_ready")
        bias_done, bias_used = sem("bias_done"), sem("bias_used")
        up_done, silu_done, hid_hi_done, hid_ready = sem("up_done"), sem("silu_done"), sem("hid_hi_done"), sem("hid_ready")
        down_done, down_used, y_ready = sem("down_done"), sem("down_used"), sem("y_ready")

        block = st.enter_context(nc.Block())

        def wait_apart(eng, semaphore, value, *more):
            pairs = [(semaphore, value), *zip(more[::2], more[1::2])]
            pairs = [(s, v if isinstance(v, int) else eng.to_reg(v)) for s, v in pairs]
            eng.wait_ge(consts_ready, 3)
            if eng is nc.scalar:
                eng.wait_ge(in_cols, 16)
            for s, v in pairs:
                eng.wait_ge(s, v)

        def v_bias(s):
            return cols[:, bass.ds(s.qo2 * 2 + (2 * IT + s.pp), 1)]

        def three(pe, o, a_hi, a_lo, b_hi, b_lo, first, last):
            pe.matmul(o, a_hi, b_hi, start=first, stop=False)
            pe.matmul(o, a_hi, b_lo, start=False, stop=False)
            return pe.matmul(o, a_lo, b_hi, start=False, stop=last)

        class Slot:

            def __init__(s, t, pl):
                s.t, s.pl = t, pl
                s.static = t * SPQ + pl if isinstance(t, int) else None
                s.first = 0 if s.static is None else s.static
                s.par = pl % 2
                s.pp = pl % 2
                s.g = (pl // 2) % G
                s.ub = (pl // 2) % 2
                full = s.static is None
                p = s.static
                s.front = full or p < SLOTS
                s.back = full or 1 <= p <= SLOTS
                s.evac_o = full or 2 <= p <= SLOTS + 1
                s.proj = full or p // 2 + 1 < UNITS
                s.oproj = s.pp == 1 and (full or p >= 3)
                s.gn = (pl // 2 + 1) % G
                s.qn = t + (pl // 2 + 1) // G
                s.qo2 = t + (pl // 2 - 1) // G
                s.go = (pl // 2 - 1) % G
                s.qo = t + (pl // 2 - 1) // G

            def n(s, per_slot, c):
                return s.t * (SPQ * per_slot) + (s.pl * per_slot + c)

            def u(s, per_unit, c):
                return s.t * (G * per_unit) + (s.pl // 2 * per_unit + c)

        def all_slots(eng, emit, behind={}):
            for p in range(3):
                emit(Slot(0, p))
                behind.get(p, lambda: None)()
            with eng.Fori(0, QUADS - 1) as t:
                for pl in range(3, 3 + SPQ):
                    emit(Slot(t, pl))
            for pl in range(3, SPQ + 2):
                emit(Slot(QUADS - 1, pl))
                behind.get((QUADS - 1) * SPQ + pl, lambda: None)()

        @block.sync
        def _(sp):
            def load_xt(b):
                src = x_t[:, slices(b, GROUP)].rearrange("(k p) n -> p k n", p=P)
                sp.dma_start(xt_raw[b], src).then_inc(in_xt[b], 16)

            load_xt(0)
            for i, part in enumerate(PARTS):
                sp.dma_start(w_raw[:, part, :, :], w_quads[0, :, part, :, :]).then_inc(in_quad[i], 16)
                if i < 2:
                    load_xt(i + 1)
            load_xt(3)
            for b in range(G):
                if b > 0:
                    sp.wait_ge(wvo_step, b)
                sp.dma_start(ex_raw[:, :, :], w_cross[b]).then_inc(in_cross, 16)
                sp.wait_ge(xt_ready, b + 1)
                sp.dma_start(xacc[:, slices(b, GT), :], x[slices(b, GROUP), :].rearrange("(t p) d -> p t d", p=P)
                             ).then_inc(in_x[b], 16)
            sp.wait_ge(wvo_step, G)
            with sp.Fori(1, QUADS) as t:
                for i, part in enumerate(PARTS):
                    sp.wait_ge(w_split[i], t)
                    src = w_quads[bass.ds(t, 1), :, part, :, :].rearrange("o p a k n -> (o p) a k n")
                    sp.dma_start(w_raw[:, part, :, :], src).then_inc(in_raw[i], 16)
                for e3 in range(EPQ):
                    e = t * EPQ + (e3 - EPQ)
                    for i in range(2):
                        src = w_experts[i, bass.ds(e, 1), :, :].rearrange("e p n -> (e p) n")
                        sp.dma_start(ex_raw[:, i, :], src).then_inc(in_ex[i], 16)
                    wait_apart(sp, ex_split[0], e + 1, ex_split[1], e + 1)
            def load_ctx(g):
                src = ctx_t_in[:, bass.ds(g * GROUP, GROUP)].rearrange("(k p) n -> p k n", p=P)
                sp.dma_start(ctx_t, src).then_inc(in_ctx, 16)

            def store(g):
                sp.wait_ge(y_ready, g + 1)
                dst = out[bass.ds(g * GROUP, GROUP), :].rearrange("(t p) d -> p t d", p=P)
                sp.dma_start(dst, yout).then_inc(out_done, 16)

            for i in range(3):
                sp.wait_ge(w_split[i], QUADS)
            load_ctx(0)
            with sp.Fori(0, G - 1) as g:
                sp.wait_ge(cross_done, g * 2 + 2)
                load_ctx(g + 1)
                store(g)
            store(G - 1)
            sp.wait_ge(out_done, 16 * G)

        @block.gpsimd
        def _(pool):
            nc.gpsimd.memset(ident[:, :], 0.0).then_inc(pool_step, 1)
            nc.gpsimd.memset(mask[:, :], 0.0).then_inc(pool_step, 1)
            pool.wait_ge(pool_step, 2)
            nc.gpsimd.affine_select(out=ident[:, :], in_=ident[:, :], compare_op=ALU.not_equal, fill=1.0, base=0,
                                    pattern=[[-1, P]], channel_multiplier=1).then_inc(consts_ready, 1)
            nc.gpsimd.affine_select(out=mask[:, :], in_=mask[:, :], compare_op=ALU.is_ge, fill=NEG, base=0,
                                    pattern=[[-1, P]], channel_multiplier=1).then_inc(consts_ready, 1)
            nc.gpsimd.iota(iota8[:, :, :], pattern=[[0, GT], [1, NE]], base=0, channel_multiplier=0,
                           allow_small_or_imprecise_dtypes=True).then_inc(consts_ready, 1)

            pool.wait_ge(in_bcast, 16)
            for b in range(G):
                tile = xacc[:, slices(b, GT), :]
                pool.wait_ge(in_x[b], 16)
                nc.gpsimd.tensor_tensor(tile, tile, bcast[:, 0:D].unsqueeze(1).to_broadcast([P, GT, D]), ALU.add
                                        ).then_inc(x_ready, 1)

            def split(hi, lo, raw, half, done):
                nc.gpsimd.tensor_copy(hi, raw).then_inc(half, 1)
                pool.wait_ge(half, done[1])
                nc.gpsimd.tensor_tensor(lo, raw, hi.bitcast(F32), ALU.subtract).then_inc(done[0], 1)

            steps_per_quad = len(PARTS) + 2 * EPQ

            def split_part(t, i, step):
                wait_apart(pool, in_raw[i], t * 16, (proj_qk, proj_v, proj_o)[i], t * (G * (4, 2, 2)[i]))
                part = PARTS[i]
                split(w_hi[:, part, :, :], w_lo[:, part, :, :], w_raw[:, part, :, :], pool_half,
                      (w_split[i], (t - 1) * steps_per_quad + step))

            with pool.Fori(1, QUADS) as t:
                split_part(t, 0, 1)
                split_part(t, 1, 2)
                for e3 in range(EPQ):
                    for i, (hi, lo) in enumerate(((up_hi, up_lo), (down_hi, down_lo))):
                        e = t * EPQ + (e3 - EPQ)
                        wait_apart(pool, in_ex[i], e * 16 + 16)
                        split(hi[:, bass.ds(e, 1), :].rearrange("p e n -> p (e n)"),
                              lo[:, bass.ds(e, 1), :].rearrange("p e n -> p (e n)"), ex_raw[:, i, :], pool_half,
                              (ex_split[i], (t - 1) * steps_per_quad + (2 * e3 + i + 3)))
                split_part(t, 2, steps_per_quad)

            with pool.Fori(0, G) as g:
                for e in range(NX):
                    pool.wait_ge(hid_hi_done, g * NX + (e + 1))
                    nc.gpsimd.tensor_tensor(hid_lo[e % 2], hid[e % 2], hid_hi[e % 2].bitcast(F32),
                                            ALU.subtract).then_inc(hid_ready, 1)

        @block.tensor
        def _(pe):
            def project_qk(part, pair, g, o):
                for k in range(KT):
                    mm = three(pe, o, w_hi[:, part, k, slices(pair, P)], w_lo[:, part, k, slices(pair, P)],
                               xt_hi[:, k, slices(g, GROUP)], xt_lo[:, k, slices(g, GROUP)], k == 0, k == KT - 1)
                mm.then_inc(proj_qk, 1)

            def project_v(half, g, o):
                for j in range(2):
                    tok = slices(g * GT + half * 2 + j, P)
                    for k in range(KT):
                        mm = three(pe, o[:, slices(j, QW)], xt_hi[:, k, tok], xt_lo[:, k, tok],
                                   w_hi[:, V, k, :], w_lo[:, V, k, :], k == 0, k == KT - 1)
                mm.then_inc(proj_v, 1)

            def project_o(half, o):
                for j in range(2):
                    tok = slices(half * 2 + j, P)
                    for k in range(KT):
                        mm = three(pe, o[:, slices(j, D)], ot_hi[:, k, tok], ot_lo[:, k, tok],
                                   w_hi[:, O, k, :], w_lo[:, O, k, :], k == 0, k == KT - 1)
                mm.then_inc(proj_o, 1)

            pe.wait_ge(xt_ready, 1)
            pe.wait_ge(w_split[0], 1)
            for f in range(4):
                if f >= 2:
                    pe.wait_ge(qk_ready, f - 1)
                project_qk((Q, K)[f // 2], f % 2, 0, pj_bank[f % 2][:, :])
            for f in range(2):
                pe.wait_ge(qk_ready, 3 + f)
                pe.wait_ge(w_split[1], 1)
                project_v(f, 0, pj_bank[f][:, :])
            pe.wait_ge(consts_ready, 3)

            def cross_weights(r):
                pe.wait_ge(in_cross, 16 * (r + 1))
                for i in range(2):
                    for m in range(KT):
                        mm = pe.matmul(bank[7][:, slices(m, D)], ex_raw[:, 0, i * D + m * P:i * D + (m + 1) * P],
                                       ex_raw[:, 1, slices(i, D)], start=(r == 0 and i == 0 and m == 0),
                                       stop=(r == G - 1 and i == 1), skip_group_check=True)
                mm.then_inc(wvo_step, 1)

            def slot(s):
                def fill(f):
                    o = pj_bank[0 if s.static == SLOTS + 1 else f % 2][:, :]
                    if s.pp == 0 and s.proj:
                        if f < 2:
                            pe.wait_ge(v_ready, s.u(2, f + 1))
                            if s.static is None or s.static >= 4:
                                pe.wait_ge(o_added, s.u(2, f - 3))
                        else:
                            pe.wait_ge(qk_ready, s.u(4, 4 + f - 1))
                        if f == 0 and s.static is not None and s.gn > 0:
                            pe.wait_ge(xt_ready, s.gn + 1)
                        if f == 0 and s.gn == 0:
                            pe.wait_ge(w_split[0], s.qn + 1)
                        project_qk((Q, K)[f // 2], f % 2, s.gn, o)
                    if s.pp == 1 and f < 2 and s.proj:
                        pe.wait_ge(qk_ready, s.u(4, 4 + 3 + f))
                        if f == 0 and s.gn == 0:
                            pe.wait_ge(w_split[1], s.qn + 1)
                        project_v(f, s.gn, o)
                    if s.oproj and f >= 2:
                        if s.proj:
                            pe.wait_ge(v_ready, s.u(2, 2 + f - 1))
                        elif s.static == SLOTS + 1 and f == 3:
                            pe.wait_ge(o_added, s.u(2, -1))
                        else:
                            pe.wait_ge(o_added, s.u(2, f - 1 - 4))
                        if f == 2:
                            pe.wait_ge(ot_ready, s.u(2, 0))
                            if s.go == 0:
                                pe.wait_ge(w_split[2], s.qo + 1)
                        project_o(f - 2, o)

                def score(h):
                    if h == 0:
                        pe.wait_ge(qk_ready, s.u(4, 4))
                    if s.first > 0 or s.static is None:
                        pe.wait_ge(masked, s.n(8, -4 + 4 * h))
                    for j in range(GT):
                        rows_h = slices(h, DH)
                        mm = pe.matmul(sc_bank[h][:, slices(j, P)], qt[s.ub][rows_h, s.pp, slices(j, P)],
                                       kt[s.ub][rows_h, s.pp, slices(j, P)], start=True, stop=True)
                    mm.then_inc(scores, 1)

                def turn(h):
                    pe.wait_ge(probs_ready, s.n(2, h - 1))
                    if s.static is None or s.static >= 2:
                        pe.wait_ge((pt_a, pt_b)[h], s.n(1, -1))
                    for j in range(GT):
                        mm = pe.transpose(tr_bank[h][:, slices(j, P)], probs[:, 1 - s.par, h, slices(j, P)], ident[:, :])
                    mm.then_inc(transposed, 1)

                if s.front:
                    score(0)
                if s.back:
                    turn(0)
                fill(0)
                if s.back:
                    turn(1)
                if s.front:
                    score(1)
                fill(1)
                fill(2)
                if s.back:
                    pe.wait_ge(pt_a, s.n(1, 0))
                    pe.wait_ge(pt_b, s.n(1, 0))
                    pe.wait_ge(v_ready, s.u(2, 2 if s.pp == 1 else 0))
                    if s.static is None or s.static >= 2:
                        pe.wait_ge(ot_ready, s.n(1, -1))
                    vb = vv[s.ub if s.pp == 1 else 1 - s.ub]
                    for j in range(GT):
                        for h in range(2):
                            c = (1 - s.pp) * P + h * DH
                            mm = pe.matmul(pv_bank[slices(h, DH), slices(j, P)], vb[:, j, c:c + DH],
                                           probs_t[:, h, slices(j, P)], start=True, stop=True)
                    mm.then_inc(pv_done, 1)
                fill(3)

            def cross(g, half):
                if half == 0:
                    pe.wait_ge(in_ctx, g * 16 + 16)
                    pe.wait_ge(wvo_ready, 1)
                if isinstance(g, int) and g == 0:
                    o = fr_bank[1]
                    if half == 1:
                        pe.wait_ge(cross_used, 1)
                else:
                    o = fr_bank[half]
                    pe.wait_ge(bias_used, g * 2)
                for j in range(2):
                    for k in range(KT):
                        mm = pe.matmul(o[:, slices(j, D)], ctx_t[:, k, slices(2 * half + j, P)], wvo[:, k, :],
                                       start=(k == 0), stop=(k == KT - 1))
                mm.then_inc(cross_done, 1)

            def x2_turn(g):
                pe.wait_ge(x2_ready, g + 1)
                if isinstance(g, int) and g == 0:
                    pe.wait_ge(o_added, 2 * UNITS - 2)
                for k in range(KT):
                    for j in range(GT):
                        mm = pe.transpose(fr_bank[k][:, slices(j, P)], x2[:, j, slices(k, P)], ident[:, :])
                mm.then_inc(x2_tp, 1)

            def route(g):
                pe.wait_ge(x2_t_ready, g * 2 + 2)
                for j in range(GT):
                    for k in range(KT):
                        mm = pe.matmul(fr_bank[0][:, slices(j, NE)], x2_t[:, k, slices(j, P)], gate[:, k, :],
                                       start=(k == 0), stop=(k == KT - 1))
                mm.then_inc(logit_done, 1)

            def comb_turn(g):
                pe.wait_ge(comb_ready, g + 1)
                for j in range(GT):
                    mm = pe.matmul(fr_bank[1][0:NX, slices(j, P)], comb[:, j, :], ident[:, :], start=True, stop=True)
                mm.then_inc(comb_tp, 1)

            def bias(g):
                pe.wait_ge(comb_t_ready, g + 1)
                for j in range(GT):
                    mm = pe.matmul(fr_bank[j // 2][:, slices(j % 2, D)], comb_t[:, slices(j, P)], down_b[:, :],
                                   start=True, stop=True)
                    if j % 2 == 1:
                        mm.then_inc(bias_done, 1)

            def up(g, e):
                if e == 0:
                    pe.wait_ge(x2_split, g + 1)
                if isinstance(g, int) and g == 0 and e < 2:
                    if e == 0:
                        pe.wait_ge(masked, 8 * SLOTS)
                        pe.wait_ge(pt_a, SLOTS)
                        pe.wait_ge(pt_b, SLOTS)
                        pe.wait_ge(ex_split[0], NX)
                        pe.wait_ge(ex_split[1], NX)
                else:
                    before = {0: 0, 1: -1}.get(e, e - 1)
                    pe.wait_ge(silu_done, g * (2 * NX) + 2 * before)
                for m in range(2):
                    for k in range(KT):
                        c = slice(k * D + m * P, k * D + (m + 1) * P)
                        cols_g = bass.ds(g * GROUP, GROUP)
                        mm = three(pe, up_bank[e % 2][m][:, :], up_hi[:, e, c], up_lo[:, e, c],
                                   xt_hi[:, k, cols_g], xt_lo[:, k, cols_g], k == 0, k == KT - 1)
                    mm.then_inc(up_done, 1)

            def down(g, e):
                pe.wait_ge(hid_ready, g * NX + (e + 1))
                for half in range(2):
                    if isinstance(g, int) and g == 0 and e == 0:
                        if half == 0:
                            pe.wait_ge(ot_ready, SLOTS)
                    else:
                        pe.wait_ge(down_used, g * (2 * NX) + (2 * e - 1 + half))
                    for j in (2 * half, 2 * half + 1):
                        for k in range(KT):
                            mm = three(pe, dn_bank[half][:, slices(j % 2, D)], hid_hi[e % 2][:, k, slices(j, P)],
                                       hid_lo[e % 2][:, k, slices(j, P)], down_hi[:, e, slices(k, D)],
                                       down_lo[:, e, slices(k, D)], k == 0, k == KT - 1)
                    mm.then_inc(down_done, 1)

            def ffn_and_front(g, front):
                for e in range(NX + LAG):
                    if e < NX:
                        up(g, e)
                    if e == 1:
                        comb_turn(g)
                    if e == 2:
                        bias(g)
                    if e >= LAG:
                        down(g, e - LAG)
                    if front and e == CROSS:
                        cross(g + 1, 0)
                        cross(g + 1, 1)
                    if front and e == X2_TURN:
                        x2_turn(g + 1)
                    if front and e == ROUTE:
                        route(g + 1)

            pe.wait_ge(in_small, 32)
            all_slots(pe, slot, {0: lambda: cross_weights(0), 1: lambda: cross_weights(1),
                                 2: lambda: (cross_weights(2), cross_weights(3)),
                                 27: lambda: cross(0, 0), 29: lambda: cross(0, 1), 31: lambda: x2_turn(0),
                                 32: lambda: route(0)})
            ffn_and_front(0, True)
            with pe.Fori(1, G - 1) as g:
                ffn_and_front(g, True)
            ffn_and_front(G - 1, False)

        @block.scalar
        def _(act):
            act.dma_start(cols[:, :], col_bias).then_inc(in_cols, 16)
            act.dma_start(bcast[:, :], row_bias.partition_broadcast(P)).then_inc(in_bcast, 16)
            act.dma_start(down_b[:, :], down_bias).then_inc(in_small, 16)
            act.dma_start(gate[:, :, :], w_gate).then_inc(in_small, 16)

            def split_xt(b):
                act.wait_ge(in_xt[b], 16)
                nc.scalar.activation(xt_hi[:, :, slices(b, GROUP)], xt_raw[b], ACT.Copy).then_inc(xt_hi_ready, 1)

            split_xt(0)

            def take_qk(f, g, quad, ub):
                dst = (qt, kt)[f // 2][ub][:, f % 2, :]
                b = cols[:, bass.ds(quad * 2 + ((f // 2) * IT + f % 2), 1)]
                nc.scalar.activation(dst, pj_bank[f % 2][:, :], ACT.Identity, bias=b).then_inc(qk_ready, 1)

            def take_wvo():
                act.wait_ge(wvo_step, G)
                nc.scalar.activation(wvo[:, :, :], bank[7][:, :].rearrange("p (k n) -> p k n", k=KT), ACT.Copy
                                     ).then_inc(wvo_ready, 1)

            def take_v(f, ub):
                nc.scalar.activation(vv[ub][:, 2 * f:2 * f + 2, :],
                                     pj_bank[f][:, :].rearrange("p (j n) -> p j n", j=2), ACT.Copy).then_inc(v_ready, 1)

            act.wait_ge(in_cols, 16)
            for f in range(4):
                act.wait_ge(proj_qk, f + 1)
                take_qk(f, 0, 0, 0)
            for f in range(2):
                act.wait_ge(proj_v, f + 1)
                take_v(f, 0)
            for b in range(1, G):
                split_xt(b)

            def slot(s):
                def take(f):
                    if s.pp == 0 and s.proj:
                        wait_apart(act, proj_qk, s.u(4, 4 + f + 1))
                        take_qk(f, s.gn, s.qn, 1 - s.ub)
                    if s.pp == 1 and f < 2 and s.proj:
                        act.wait_ge(proj_v, s.u(2, 2 + f + 1))
                        take_v(f, 1 - s.ub)

                def exps(h):
                    for j in range(GT):
                        act.wait_ge(masked, s.n(8, 4 * h + j + 1))
                        tile = probs[:, s.par, h, slices(j, P)]
                        nc.scalar.activation(tile, tile, ACT.Exp, scale=-1.0, bias=negmax[:, s.par, h, j:j + 1],
                                             accum_out=sums[:, s.par, h, j:j + 1]).then_inc(exped, 1)

                if s.evac_o:
                    waits = (pv_done, s.n(1, -1))
                    if s.pp == 0 and (s.static is None or s.static >= 4):
                        waits += (proj_o, s.u(2, -2))
                    wait_apart(act, *waits)
                    nc.scalar.activation(ot_hi[:, s.pp, :], pv_bank[:, :], ACT.Identity, bias=v_bias(s)
                                         ).then_inc(ot_hi_ready, 1)
                if s.front:
                    exps(0)
                take(0)
                if s.back:
                    act.wait_ge(transposed, s.n(2, 0))
                    nc.scalar.activation(probs_t[:, 1, :], tr_bank[1][:, :], ACT.Copy).then_inc(pt_b, 1)
                if s.front:
                    exps(1)
                take(1)
                take(2)
                take(3)

            def root1(g):
                act.wait_ge(var_ready, g * 2 + 1)
                nc.scalar.activation(std[:, :], mv[:, :, 1], ACT.Sqrt, bias=eps[:, 0:1]).then_inc(std_ready, 1)

            def root2(g):
                act.wait_ge(var_ready, g * 2 + 2)
                nc.scalar.activation(std[:, :], mv[:, :, 1], ACT.Sqrt, bias=eps[:, 0:1]).then_inc(std_ready, 1)

            def take_x2(g):
                act.wait_ge(x2_tp, g + 1)
                for k in range(KT):
                    nc.scalar.activation(x2_t[:, k, :], fr_bank[k][:, :], ACT.Copy).then_inc(x2_t_ready, 1)

            def route_exp(g):
                act.wait_ge(shift_ready, g + 1)
                nc.scalar.activation(expd[:, :, :], shifted[:, :, :], ACT.Exp).then_inc(exp_ready, 1)

            def take_comb(g):
                act.wait_ge(comb_tp, g + 1)
                nc.scalar.activation(comb_t[:, :], fr_bank[1][0:NX, :], ACT.Copy).then_inc(comb_t_ready, 1)

            def hidden(g, e):
                if not (isinstance(g, int) and g == 0 and e < 2):
                    before = {0: 0, 1: -1}.get(e, e - 1)
                    act.wait_ge(hid_ready, g * NX + before)
                for m in range(2):
                    act.wait_ge(up_done, g * (2 * NX) + (2 * e + m + 1))
                    b = 3 * IT + 2 * e + m
                    nc.scalar.activation(hid[e % 2][:, m, :], up_bank[e % 2][m][:, :], ACT.Silu,
                                         bias=cols[:, b:b + 1]).then_inc(silu_done, 1)
                if not (isinstance(g, int) and g == 0 and e < 2):
                    act.wait_ge(down_done, g * (2 * NX) + 2 * before)
                act.wait_ge(silu_done, g * (2 * NX) + (2 * e + 2))
                nc.scalar.activation(hid_hi[e % 2], hid[e % 2], ACT.Copy).then_inc(hid_hi_done, 1)

            def ffn_and_front(g, front):
                for e in range(NX):
                    hidden(g, e)
                    if e == 1:
                        take_comb(g)
                    if front and e == 2:
                        root1(g + 1)
                    if front and e == CROSS + 1:
                        root2(g + 1)
                    if front and e == X2_TURN:
                        take_x2(g + 1)
                    if front and e == ROUTE:
                        route_exp(g + 1)
                act.wait_ge(var3_ready, g + 1)
                nc.scalar.activation(std3[:, :], mv3[:, :, 1], ACT.Sqrt, bias=eps[:, 0:1]).then_inc(std3_ready, 1)

            all_slots(act, slot, {2: take_wvo, 27: lambda: root1(0), 30: lambda: root2(0), 31: lambda: take_x2(0),
                                  33: lambda: route_exp(0)})
            ffn_and_front(0, True)
            with act.Fori(1, G - 1) as g:
                ffn_and_front(g, True)
            ffn_and_front(G - 1, False)

        @block.vector
        def _(dve):
            nc.vector.memset(eps[:, :], EPS).then_inc(dve_step, 1)
            nc.vector.memset(comb[:, :, :], 1.0).then_inc(dve_step, 1)
            def split_xt(b):
                dve.wait_ge(xt_hi_ready, b + 1)
                hi = xt_hi[:, :, slices(b, GROUP)]
                nc.vector.tensor_tensor(xt_lo[:, :, slices(b, GROUP)], xt_raw[b], hi.bitcast(F32),
                                        ALU.subtract).then_inc(xt_ready, 1)

            def split_part(i):
                part = PARTS[i]
                dve.wait_ge(in_quad[i], 16)
                nc.vector.tensor_copy(w_hi[:, part, :, :], w_raw[:, part, :, :]).then_inc(dve_step, 1)
                dve.wait_ge(dve_step, 3 + i)
                nc.vector.tensor_tensor(w_lo[:, part, :, :], w_raw[:, part, :, :], w_hi[:, part, :, :].bitcast(F32),
                                        ALU.subtract).then_inc(w_split[i], 1)

            split_xt(0)
            split_part(0)
            split_part(1)
            split_xt(1)
            split_part(2)
            split_xt(2)
            split_xt(3)
            dve.wait_ge(consts_ready, 3)

            def slot(s):
                def mask_and_max(h):
                    wait_apart(dve, scores, s.n(2, h + 1))
                    for j in range(GT):
                        nc.vector.tensor_tensor_reduce(
                            probs[:, s.par, h, slices(j, P)], sc_bank[h][:, slices(j, P)], mask[:, :], -SCALE, 3.0e38,
                            ALU.add, ALU.min, negmax[:, s.par, h, j:j + 1]).then_inc(masked, 1)

                def normalise(h):
                    dve.wait_ge(exped, s.n(8, 4 * h + 4))
                    nc.vector.reciprocal(rsum[:, h, :], sums[:, s.par, h, :]).then_inc(rsum_ready, 1)
                    dve.wait_ge(rsum_ready, s.n(2, h + 1))
                    tile = probs[:, s.par, h, :].rearrange("p (j k) -> p j k", j=GT)
                    nc.vector.tensor_tensor(tile, tile, rsum[:, h, :].unsqueeze(2).to_broadcast([P, GT, P]), ALU.mult
                                            ).then_inc(probs_ready, 1)

                def add_o(half):
                    dve.wait_ge(proj_o, s.u(2, half - 1))
                    if half == 0 and s.static is None:
                        dve.wait_ge(x_ready, s.go + 1)
                    o = pj_bank[0 if s.static == SLOTS + 1 else half]
                    tile = xacc[:, s.go * GT + 2 * half:s.go * GT + 2 * half + 2, :]
                    nc.vector.tensor_tensor(tile, o[:, :].rearrange("p (j n) -> p j n", j=2), tile,
                                            ALU.add).then_inc(o_added, 1)

                if s.evac_o:
                    dve.wait_ge(ot_hi_ready, s.n(1, -1))
                    nc.vector.scalar_tensor_tensor(out=ot_lo[:, s.pp, :], in0=pv_bank[:, :], scalar=v_bias(s),
                                                   in1=ot_hi[:, s.pp, :].bitcast(F32), op0=ALU.add,
                                                   op1=ALU.subtract).then_inc(ot_ready, 1)
                if s.front:
                    mask_and_max(0)
                if s.back:
                    dve.wait_ge(transposed, s.n(2, -1))
                    nc.vector.tensor_copy(probs_t[:, 0, :], tr_bank[0][:, :]).then_inc(pt_a, 1)
                if s.front:
                    normalise(0)
                    mask_and_max(1)
                if s.oproj:
                    add_o(0)
                if s.front:
                    normalise(1)
                if s.oproj:
                    add_o(1)

            class Chain:
                per_body = BODY_STEPS
                c, g = 5, 0

                def step(s, ins, wait=lambda eng, semaphore, value: eng.wait_ge(semaphore, value)):
                    s.c += 1
                    ins.then_inc(dve_step, 1)
                    wait(dve, dve_step, s.g * s.per_body + s.c)

            ch = Chain()

            def statistics(src, st6, m, ready):
                for j in range(GT):
                    last = nc.vector.bn_stats(st6[:, j, :], src(j))
                ch.step(last, wait_apart)
                for j in range(GT):
                    last = nc.vector.bn_aggr(m[:, j, :], st6[:, j, :])
                last.then_inc(ready, 1)

            def apply(src, dst, m, root, r):
                ch.step(nc.vector.reciprocal(r[:, :], root[:, :]))
                for j in range(GT):
                    last = nc.vector.tensor_scalar(dst[:, j, :], src(j), m[:, j, 0:1], r[:, j:j + 1],
                                                   ALU.subtract, ALU.mult)
                return last

            def tile_of(g):
                def src(j):
                    return xacc[:, bass.ds(g * GT + j, 1), :].rearrange("p t n -> p (t n)")
                return src

            def norm1_stats(g):
                if isinstance(g, int) and g == 0:
                    dve.wait_ge(o_added, 2 * (UNITS - G + 1))
                statistics(tile_of(g), stats, mv, var_ready)

            def norm1(g):
                dve.wait_ge(std_ready, g * 2 + 1)
                ch.step(apply(tile_of(g), x1, mv, std, rstd))
                ch.step(nc.vector.tensor_tensor(x1, x1, bcast[:, D:2 * D].unsqueeze(1).to_broadcast([P, GT, D]),
                                                ALU.add))

            def add_cross(g, half):
                dve.wait_ge(cross_done, g * 2 + (half + 1))
                tile = x1[:, 2 * half:2 * half + 2, :]
                o = fr_bank[1 if isinstance(g, int) and g == 0 else half]
                nc.vector.tensor_tensor(tile, o[:, :].rearrange("p (j n) -> p j n", j=2), tile, ALU.add
                                        ).then_inc(cross_used, 1)

            def norm2_stats(g):
                dve.wait_ge(cross_used, g * 2 + 2)
                statistics(lambda j: x1[:, j, :], stats, mv, var_ready)

            def norm2(g):
                dve.wait_ge(std_ready, g * 2 + 2)
                apply(lambda j: x1[:, j, :], x2, mv, std, rstd).then_inc(x2_ready, 1)

            def split_x2(g):
                dve.wait_ge(x2_t_ready, g * 2 + 2)
                cols_g = bass.ds(g * GROUP, GROUP)
                ch.step(nc.vector.tensor_copy(xt_hi[:, :, cols_g], x2_t))
                nc.vector.tensor_tensor(xt_lo[:, :, cols_g], x2_t, xt_hi[:, :, cols_g].bitcast(F32), ALU.subtract
                                        ).then_inc(x2_split, 1)

            def best_two(g):
                dve.wait_ge(logit_done, g + 1)
                ch.step(nc.vector.tensor_copy(logits[:, :, :],
                                              fr_bank[0][:, 0:GT * NE].rearrange("p (j e) -> p j e", j=GT)),
                        wait_apart)
                for j in range(GT):
                    last = nc.vector.max(top8[:, j, :], logits[:, j, :])
                ch.step(last)
                top = top8[:, :, 0:1]
                nc.vector.tensor_tensor(shifted[:, :, 0:NE], logits[:, :, :], top.to_broadcast([P, GT, NE]), ALU.subtract)
                nc.vector.tensor_tensor(shifted[:, :, NE:NE + 2], top8[:, :, 0:2], top.to_broadcast([P, GT, 2]),
                                        ALU.subtract).then_inc(shift_ready, 1)
                for j in range(GT):
                    last = nc.vector.max_index(idx8[:, j, :], top8[:, j, :], logits[:, j, :])
                ch.step(last)
                ch.step(nc.vector.tensor_copy(idx2[:, :, :], idx8[:, :, 0:2]))
                for i in range(2):
                    last = nc.vector.tensor_tensor(hot[:, i, :, :], iota8[:, :, :],
                                                   idx2[:, :, i:i + 1].to_broadcast([P, GT, NE]), ALU.is_equal)
                ch.step(last)

            def weigh(g):
                dve.wait_ge(exp_ready, g + 1)
                ch.step(nc.vector.tensor_reduce(zsum[:, :], expd[:, :, 0:NE], AX.X, ALU.add))
                ch.step(nc.vector.reciprocal(rz[:, :], zsum[:, :]))
                ch.step(nc.vector.tensor_tensor(best[:, :, :], expd[:, :, NE:NE + 2],
                                                rz[:, :].unsqueeze(2).to_broadcast([P, GT, 2]), ALU.mult))
                ch.step(nc.vector.tensor_reduce(bsum[:, :], best[:, :, :], AX.X, ALU.add))
                ch.step(nc.vector.tensor_scalar(bsum[:, :], bsum[:, :], 1e-20, None, ALU.add))
                ch.step(nc.vector.reciprocal(rb[:, :], bsum[:, :]))
                ch.step(nc.vector.tensor_tensor(wbest[:, :, :], best[:, :, :],
                                                rb[:, :].unsqueeze(2).to_broadcast([P, GT, 2]), ALU.mult))
                for i in range(2):
                    last = nc.vector.tensor_tensor(hot[:, i, :, :], hot[:, i, :, :],
                                                   wbest[:, :, i:i + 1].to_broadcast([P, GT, NE]), ALU.mult)
                ch.step(last)
                nc.vector.tensor_tensor(comb[:, :, 0:NE], hot[:, 0, :, :], hot[:, 1, :, :], ALU.add
                                        ).then_inc(comb_ready, 1)

            def start_y(g):
                dve.wait_ge(comb_ready, g + 1)
                nc.vector.tensor_copy(comb_f[:, :, :], comb[:, :, :])
                if not (isinstance(g, int) and g == 0):
                    dve.wait_ge(y_ready, g)
                for half in range(2):
                    dve.wait_ge(bias_done, g * 2 + (half + 1))
                    nc.vector.tensor_tensor(yacc[:, 2 * half:2 * half + 2, :],
                                            fr_bank[half][:, :].rearrange("p (j n) -> p j n", j=2),
                                            x2[:, 2 * half:2 * half + 2, :], ALU.add).then_inc(bias_used, 1)
                dve.wait_ge(bias_used, g * 2 + 2)

            def add_expert(g, e):
                for half in range(2):
                    dve.wait_ge(down_done, g * (2 * NX) + (2 * e + half + 1))
                    if e > 0:
                        dve.wait_ge(down_used, g * (2 * NX) + (2 * e - 1 + half))
                    for j in (2 * half, 2 * half + 1):
                        last = nc.vector.scalar_tensor_tensor(
                            out=yacc[:, j, :], in0=dn_bank[half][:, slices(j % 2, D)], scalar=comb_f[:, j, e:e + 1],
                            in1=yacc[:, j, :], op0=ALU.mult, op1=ALU.add)
                    last.then_inc(down_used, 1)

            def finish(g):
                dve.wait_ge(down_used, g * (2 * NX) + 2 * NX)
                statistics(lambda j: yacc[:, j, :], stats3, mv3, var3_ready)
                dve.wait_ge(std3_ready, g + 1)
                if not (isinstance(g, int) and g == 0):
                    dve.wait_ge(out_done, g * 16)
                apply(lambda j: yacc[:, j, :], yout, mv3, std3, rstd3).then_inc(y_ready, 1)

            def ffn_and_front(g, front):
                ch.g, ch.c = g, FRONT_STEPS
                if front:
                    norm1_stats(g + 1)
                start_y(g)
                if front:
                    norm1(g + 1)
                for e in range(LAG, NX + LAG):
                    add_expert(g, e - LAG)
                    if front and e == CROSS:
                        add_cross(g + 1, 0)
                        add_cross(g + 1, 1)
                        norm2_stats(g + 1)
                    if front and e == CROSS + 1:
                        norm2(g + 1)
                    if front and e == X2_TURN:
                        split_x2(g + 1)
                    if front and e == ROUTE:
                        best_two(g + 1)
                    if front and e == ROUTE + 1:
                        weigh(g + 1)
                finish(g)
                if front:
                    ch.c - FRONT_STEPS == BODY_STEPS or fail(ch.c - FRONT_STEPS)

            def fail(n):
                raise ValueError(f"{n} steps of VectorE per group")

            all_slots(dve, slot, {27: lambda: norm1_stats(0), 28: lambda: (norm1(0), add_cross(0, 0)),
                                  30: lambda: (add_cross(0, 1), norm2_stats(0)), 31: lambda: norm2(0), 32: lambda: split_x2(0),
                                  33: lambda: (best_two(0), weigh(0))})
            dve.wait_ge(o_added, 2 * UNITS)
            ch.c == FRONT_STEPS or fail(ch.c)
            ffn_and_front(0, True)
            with dve.Fori(1, G - 1) as g:
                ffn_and_front(g, True)
            ffn_and_front(G - 1, False)


def kernel(**inputs):
    import numpy as np
    import concourse.bacc as bacc
    from concourse.bass_utils import run_bass_kernel_spmd

    a = {k: np.asarray(v) for k, v in inputs.items()}

    def heads_in(w):
        return w.reshape(QUADS, 4, KT, P, DH).transpose(0, 3, 2, 1, 4).reshape(QUADS, P, KT, QW)

    w_o = a["L0_attn_O_w"].reshape(INNER, D)
    o_quads = w_o.reshape(QUADS, KT, P, D).transpose(0, 2, 1, 3)
    w_v_t = a["L0_xattn_Wkv"][:, INNER:].T
    w_out = a["L0_xattn_Wout"]
    up = np.concatenate([a["L0_ffn_up_w"], a["L0_ffn_sh_up_w"][None]])
    down = np.concatenate([a["L0_ffn_down_w"], a["L0_ffn_sh_down_w"][None]])
    up_b = np.concatenate([a["L0_ffn_up_b"], a["L0_ffn_sh_up_b"][None]])

    def by_partition(w):
        return w.reshape(NX, KT, P, D).transpose(0, 2, 1, 3).reshape(NX, P, KT * D)

    arrays = {
        "x": a["x"].reshape(TOK, D),
        "x_t": a["x"].reshape(TOK, D).T,
        "ctx_t_in": a["ctx_1024"].reshape(TOK, D).T,
        "w_quads": np.stack([heads_in(a["L0_attn_Q_w"]), heads_in(a["L0_attn_K_w"]), heads_in(a["L0_attn_V_w"]),
                             o_quads], axis=2),
        "w_cross": np.concatenate([w_v_t.reshape(4, 1, 2, P, D), w_out.reshape(4, 1, 2, P, D)], axis=1
                                  ).transpose(0, 3, 1, 2, 4).reshape(4, P, 2, 2 * D),
        "w_experts": np.stack([by_partition(up), by_partition(down)]),
        "w_gate": a["L0_ffn_gate_w"].T.reshape(KT, P, NE).transpose(1, 0, 2),
        "col_bias": np.concatenate([a[f"L0_attn_{n}_b"].reshape(IT, P).T for n in "QKV"]
                                   + [up_b.reshape(2 * NX, P).T], axis=1),
        "row_bias": np.concatenate([a["L0_attn_O_b"], a["L0_xattn_bout"]]),
        "down_bias": np.concatenate([a["L0_ffn_down_b"], a["L0_ffn_sh_down_b"][None]]),
    }
    arrays = {k: np.ascontiguousarray(v) for k, v in arrays.items()}
    nc = bacc.Bacc("TRN2", target_bir_lowering=False, num_devices=1)
    aps = {k: nc.dram_tensor(f"in_{k}", v.shape, F32, kind="ExternalInput").ap() for k, v in arrays.items()}
    out = nc.dram_tensor("out_0", (TOK, D), F32, kind="ExternalOutput").ap()
    decoder_program(nc, out=out, **aps)
    r = run_bass_kernel_spmd(nc, [{f"in_{k}": v for k, v in arrays.items()}], core_ids=[0])
    return r.results[0]["out_0"].reshape(SEQS, S, D)
```

```python
from contextlib import ExitStack

import concourse.bass as bass
from concourse import mybir

F32 = mybir.dt.float32
F32R = mybir.dt.float32r
U32 = mybir.dt.uint32
I32 = mybir.dt.int32
ALU = mybir.AluOpType
ACT = mybir.ActivationFunctionType
AX = mybir.AxisListType

P = 128
SEQS, S, D = 16, 128, 256
HEADS, DH = 16, 64
TOK = SEQS * S
KT = D // P
GROUP = 512
G = TOK // GROUP
GT = GROUP // P
QUADS = HEADS // 4
UNITS = QUADS * G
SLOTS = 2 * UNITS
SPQ = 2 * G
QW = 4 * DH
NX = 9
NE = 8
SCALE = DH ** -0.5
NEG = -1.0e30
EPS = 1e-5
ROOT_GUESS = float(0x5f3759df)
NEWTON = 3
WARM_UP = 12
INNER = HEADS * DH
IT = INNER // P

Q, K, V, O = range(4)
PARTS = (slice(Q, V), slice(V, O), slice(O, O + 1))
EPQ = NX // (QUADS - 1)
LAG = 2
CROSS, X2_TURN, ROUTE = 3, 5, 6
FRONT_STEPS = 20
BODY_STEPS = 41
FRONT, LAST, BOTH = slice(0, 1), slice(1, 2), slice(0, 2)
HALVES = 2 * NX - 1


def slices(i, n):
    return slice(i * n, (i + 1) * n)


def decoder_program(nc, x, x_t, ctx_t_in, w_quads, w_cross, w_experts, w_gate, col_bias, row_bias, down_bias,
                    out):
    st = ExitStack()
    with st:
        def sb(name, shape, dt=F32):
            return st.enter_context(nc.sbuf_tensor(name, shape, dt))

        def sem(name):
            return st.enter_context(nc.semaphore(name))

        xt_hi = sb("xt_hi", [P, KT, TOK], F32R)
        xt_lo = sb("xt_lo", [P, KT, TOK], F32R)
        xacc = sb("xacc", [P, TOK // P, D])
        w_raw = sb("w_raw", [P, 4, KT, QW])
        w_hi = sb("w_hi", [P, 4, KT, QW], F32R)
        w_lo = sb("w_lo", [P, 4, KT, QW], F32R)
        qkv = sb("qkv", [P, 12 * GROUP])
        probs = sb("probs", [P, 2, 2, GROUP])
        probs_t = sb("probs_t", [P, 2, GROUP])
        ot_hi = sb("ot_hi", [P, 2, GROUP], F32R)
        ot_lo = sb("ot_lo", [P, 2, GROUP], F32R)
        up_hi = sb("up_hi", [P, NX, KT * D], F32R)
        up_lo = sb("up_lo", [P, NX, KT * D], F32R)
        down_hi = sb("down_hi", [P, NX, KT * D], F32R)
        down_lo = sb("down_lo", [P, NX, KT * D], F32R)
        ex_raw = sb("ex_raw", [P, 2, KT * D])
        wvo = sb("wvo", [P, KT, D])
        gate = sb("gate", [P, KT, NE])
        cols = sb("cols", [P, 2 * IT + IT + 2 * NX])
        bcast = sb("bcast", [P, 2 * D])
        down_b = sb("down_b", [NX, D])
        ident = sb("ident", [P, P])
        mask = sb("mask", [P, P])
        negmax = sb("negmax", [P, 2, 2, GT])
        sums = sb("sums", [P, 2, 2, GT])
        rsum = sb("rsum", [P, 2, GT])
        iota8 = sb("iota8", [P, GT, NE])
        stats = sb("stats", [P, 2, GT, 6])
        mv = sb("mv", [P, 2, GT, 2])
        rstd = sb("rstd", [P, 2, GT])
        var_eps = sb("var_eps", [P, 2, GT])
        root_sq = sb("root_sq", [P, 2, GT])
        logits = sb("logits", [P, GT, NE])
        top8 = sb("top8", [P, GT, 8])
        idx8 = sb("idx8", [P, GT, 8], U32)
        idx2 = sb("idx2", [P, GT, 2])
        shifted = sb("shifted", [P, GT, NE + 2])
        expd = sb("expd", [P, GT, NE + 2])
        zsum = sb("zsum", [P, GT])
        rz = sb("rz", [P, GT])
        best = sb("best", [P, GT, 2])
        bsum = sb("bsum", [P, GT])
        rb = sb("rb", [P, GT])
        wbest = sb("wbest", [P, GT, 2])
        hot = sb("hot", [P, 2, GT, NE])
        comb = sb("comb", [P, GT, NX])
        comb_f = sb("comb_f", [P, GT, NX])
        comb_t = sb("comb_t", [NX, GROUP])

        qt = [qkv[:, (2 * b) * GROUP:(2 * b + 2) * GROUP].rearrange("p (a n) -> p a n", a=2) for b in range(2)]
        kt = [qkv[:, (4 + 2 * b) * GROUP:(6 + 2 * b) * GROUP].rearrange("p (a n) -> p a n", a=2) for b in range(2)]
        vv = [qkv[:, (8 + 2 * b) * GROUP:(10 + 2 * b) * GROUP].rearrange("p (t n) -> p t n", t=GT) for b in range(2)]
        xt_raw = [xacc[:, slices(b, GT), :].rearrange("p t n -> p (t n)").rearrange("p (k n) -> p k n", k=KT)
                  for b in range(G)]
        w_flat = w_raw[:, :, :, :].rearrange("p a k n -> p (a k n)")
        x1 = w_flat[:, 0:2 * GROUP].rearrange("p (t n) -> p t n", t=GT)
        ctx_t = w_flat[:, 2 * GROUP:4 * GROUP].rearrange("p (k n) -> p k n", k=KT)
        x2 = qkv[:, 0:2 * GROUP].rearrange("p (t n) -> p t n", t=GT)
        x2_t = qkv[:, 4 * GROUP:6 * GROUP].rearrange("p (k n) -> p k n", k=KT)
        yacc = qkv[:, 2 * GROUP:4 * GROUP].rearrange("p (t n) -> p t n", t=GT)
        hid = [probs[:, b, :, :] for b in range(2)]
        yout = probs_t[:, :, :].rearrange("p a n -> p (a n)").rearrange("p (t n) -> p t n", t=GT)
        hid_hi = [w_hi[:, 0:2, :, :].rearrange("p a k n -> p a (k n)"), ot_hi[:, :, :]]
        hid_lo = [w_lo[:, 0:2, :, :].rearrange("p a k n -> p a (k n)"), ot_lo[:, :, :]]

        bank = [st.enter_context(nc.psum_tensor(f"bank{i}", [P, GROUP], F32)) for i in range(8)]
        sc_bank = bank[0:2]
        tr_bank = bank[2:4]
        pv_bank = bank[4]
        pj_bank = bank[5:7]
        up_bank = [bank[0:2], bank[2:4]]
        dn_bank = bank[4:6]
        fr_bank = bank[6:8]

        in_xt = [sem(f"in_xt{b}") for b in range(G)]
        in_x = [sem(f"in_x{b}") for b in range(G)]
        in_xt0 = [sem(f"in_xt0_k{k}") for k in range(KT)]
        in_quad = [sem(f"in_quad_{n}") for n in "qkvo"]
        q_split, table_ready = sem("q_split"), sem("table_ready")
        in_cols, in_bcast, in_small, in_cross = sem("in_cols"), sem("in_bcast"), sem("in_small"), sem("in_cross")
        in_raw = [sem("in_raw_qk"), sem("in_raw_v"), sem("in_raw_o")]
        in_ex = [sem("in_up"), sem("in_down")]
        in_ctx, out_done = sem("in_ctx"), sem("out_done")
        consts_ready = sem("consts_ready")
        pool_step, pool_half = sem("pool_step"), sem("pool_half")
        xt_hi_ready, xt_ready, x_ready = sem("xt_hi_ready"), sem("xt_ready"), sem("x_ready")
        wvo_step, wvo_ready = sem("wvo_step"), sem("wvo_ready")
        w_split = [sem("w_split_qk"), sem("w_split_v"), sem("w_split_o")]
        ex_split = [sem("up_split"), sem("down_split")]
        proj_qk, proj_v, proj_o = sem("proj_qk"), sem("proj_v"), sem("proj_o")
        qk_ready, v_ready, o_added = sem("qk_ready"), sem("v_ready"), sem("o_added")
        scores, masked, exped = sem("scores"), sem("masked"), sem("exped")
        rsum_ready, probs_ready = sem("rsum_ready"), sem("probs_ready")
        transposed, pt_a, pt_b = sem("transposed"), sem("pt_a"), sem("pt_b")
        pv_done, ot_hi_ready, ot_ready = sem("pv_done"), sem("ot_hi_ready"), sem("ot_ready")
        dve_step = sem("dve_step")
        var_ready, rstd_ready, root_step = sem("var_ready"), sem("rstd_ready"), sem("root_step")
        x1_ready, bout_added = sem("x1_ready"), sem("bout_added")
        cross_done, cross_used = sem("cross_done"), sem("cross_used")
        x2_ready, x2_tp, x2_t_ready, x2_split = sem("x2_ready"), sem("x2_tp"), sem("x2_t_ready"), sem("x2_split")
        x2_hi_ready = sem("x2_hi_ready")
        logit_done, shift_ready, exp_ready, comb_ready = (sem("logit_done"), sem("shift_ready"),
                                                          sem("exp_ready"), sem("comb_ready"))
        comb_tp, comb_t_ready = sem("comb_tp"), sem("comb_t_ready")
        bias_done, bias_used = sem("bias_done"), sem("bias_used")
        up_done, silu_done, hid_hi_done, hid_ready = sem("up_done"), sem("silu_done"), sem("hid_hi_done"), sem("hid_ready")
        hid_last_ready = sem("hid_last_ready")
        down_done, down_used, y_ready = sem("down_done"), sem("down_used"), sem("y_ready")

        block = st.enter_context(nc.Block())

        def wait_apart(eng, semaphore, value, *more):
            pairs = [(semaphore, value), *zip(more[::2], more[1::2])]
            pairs = [(s, v if isinstance(v, int) else eng.to_reg(v)) for s, v in pairs]
            eng.wait_ge(consts_ready, 3)
            if eng is nc.scalar:
                eng.wait_ge(in_cols, 16)
            for s, v in pairs:
                eng.wait_ge(s, v)

        def v_bias(s):
            return cols[:, bass.ds(s.qo2 * 2 + (2 * IT + s.pp), 1)]

        def three(pe, o, a_hi, a_lo, b_hi, b_lo, first, last):
            pe.matmul(o, a_hi, b_hi, start=first, stop=False)
            pe.matmul(o, a_hi, b_lo, start=False, stop=False)
            return pe.matmul(o, a_lo, b_hi, start=False, stop=last)

        def inverse_root(eng, which, step):
            v, r, q = var_eps[:, which, :], rstd[:, which, :], root_sq[:, which, :]
            step(eng.tensor_scalar(v, mv[:, which, :, 1], EPS, None, ALU.add))
            step(eng.tensor_scalar(r.bitcast(I32), v.bitcast(I32), -0.5, ROOT_GUESS, ALU.mult, ALU.add))
            for _ in range(NEWTON):
                step(eng.tensor_tensor(q, r, r, ALU.mult))
                if eng is nc.vector:
                    step(eng.scalar_tensor_tensor(out=q, in0=q, scalar=-0.5, in1=v, op0=ALU.mult, op1=ALU.mult))
                    step(eng.scalar_tensor_tensor(out=r, in0=q, scalar=1.5, in1=r, op0=ALU.add, op1=ALU.mult))
                else:
                    step(eng.tensor_tensor(q, q, v, ALU.mult))
                    step(eng.tensor_scalar(q, q, -0.5, 1.5, ALU.mult, ALU.add))
                    step(eng.tensor_tensor(r, r, q, ALU.mult))

        class Slot:

            def __init__(s, t, pl):
                s.t, s.pl = t, pl
                s.static = t * SPQ + pl if isinstance(t, int) else None
                s.first = 0 if s.static is None else s.static
                s.par = pl % 2
                s.pp = pl % 2
                s.g = (pl // 2) % G
                s.ub = (pl // 2) % 2
                full = s.static is None
                p = s.static
                s.front = full or p < SLOTS
                s.back = full or 1 <= p <= SLOTS
                s.evac_o = full or 2 <= p <= SLOTS + 1
                s.proj = full or p // 2 + 1 < UNITS
                s.oproj = s.pp == 1 and (full or p >= 3)
                s.gn = (pl // 2 + 1) % G
                s.qn = t + (pl // 2 + 1) // G
                s.qo2 = t + (pl // 2 - 1) // G
                s.go = (pl // 2 - 1) % G
                s.qo = t + (pl // 2 - 1) // G
                s.act_turns = s.static is not None and SLOTS - 2 <= s.static <= SLOTS
                s.o_bank = {SLOTS - 1: (bank[5], bank[5]), SLOTS + 1: (bank[5], bank[4])}.get(s.static, bank[5:7])

            def n(s, per_slot, c):
                return s.t * (SPQ * per_slot) + (s.pl * per_slot + c)

            def u(s, per_unit, c):
                return s.t * (G * per_unit) + (s.pl // 2 * per_unit + c)

        def all_slots(eng, emit, behind={}):
            for p in range(3):
                emit(Slot(0, p))
                behind.get(p, lambda: None)()
            with eng.Fori(0, QUADS - 1) as t:
                for pl in range(3, 3 + SPQ):
                    emit(Slot(t, pl))
            for pl in range(3, SPQ + 2):
                emit(Slot(QUADS - 1, pl))
                behind.get((QUADS - 1) * SPQ + pl, lambda: None)()

        @block.sync
        def _(sp):
            def load_xt(b):
                src = x_t[:, slices(b, GROUP)].rearrange("(k p) n -> p k n", p=P)
                sp.dma_start(xt_raw[b], src).then_inc(in_xt[b], 16)

            for part in (Q, K, V, O):
                sp.dma_start(w_raw[:, part, :, :], w_quads[0, :, part, :, :]).then_inc(in_quad[part], 16)
                if part == Q:
                    for k in range(KT):
                        sp.dma_start(xt_raw[0][:, k, :], x_t[slices(k, P), 0:GROUP]).then_inc(in_xt0[k], 16)
                if part >= V:
                    load_xt(part - V + 1)
            load_xt(3)
            for b in range(G):
                if b > 0:
                    sp.wait_ge(wvo_step, b)
                sp.dma_start(ex_raw[:, :, :], w_cross[b]).then_inc(in_cross, 16)
                sp.wait_ge(xt_ready, b + 1)
                sp.dma_start(xacc[:, slices(b, GT), :], x[slices(b, GROUP), :].rearrange("(t p) d -> p t d", p=P)
                             ).then_inc(in_x[b], 16)
            sp.wait_ge(wvo_step, G)
            with sp.Fori(1, QUADS) as t:
                for i, part in enumerate(PARTS):
                    sp.wait_ge(w_split[i], t)
                    src = w_quads[bass.ds(t, 1), :, part, :, :].rearrange("o p a k n -> (o p) a k n")
                    sp.dma_start(w_raw[:, part, :, :], src).then_inc(in_raw[i], 16)
                for e3 in range(EPQ):
                    e = t * EPQ + (e3 - EPQ)
                    for i in range(2):
                        src = w_experts[i, bass.ds(e, 1), :, :].rearrange("e p n -> (e p) n")
                        sp.dma_start(ex_raw[:, i, :], src).then_inc(in_ex[i], 16)
                    wait_apart(sp, ex_split[0], e + 1, ex_split[1], e + 1)
            def load_ctx(g):
                src = ctx_t_in[:, bass.ds(g * GROUP, GROUP)].rearrange("(k p) n -> p k n", p=P)
                sp.dma_start(ctx_t, src).then_inc(in_ctx, 16)

            def store(g):
                if isinstance(g, int):
                    for half in range(2):
                        sp.wait_ge(y_ready, g + 1 + half)
                        dst = out[g * GROUP + half * 2 * P:g * GROUP + (half + 1) * 2 * P, :]
                        sp.dma_start(dst.rearrange("(t p) d -> p t d", p=P), yout[:, 2 * half:2 * half + 2, :]
                                     ).then_inc(out_done, 16)
                    return
                sp.wait_ge(y_ready, g + 1)
                dst = out[bass.ds(g * GROUP, GROUP), :].rearrange("(t p) d -> p t d", p=P)
                sp.dma_start(dst, yout).then_inc(out_done, 16)

            for i in range(3):
                sp.wait_ge(w_split[i], QUADS)
            load_ctx(0)
            with sp.Fori(0, G - 1) as g:
                sp.wait_ge(cross_done, g * 2 + 2)
                load_ctx(g + 1)
                store(g)
            store(G - 1)
            sp.wait_ge(out_done, 16 * (G + 2))

        @block.gpsimd
        def _(pool):
            nc.gpsimd.memset(ident[:, :], 0.0).then_inc(pool_step, 1)
            nc.gpsimd.memset(mask[:, :], 0.0).then_inc(pool_step, 1)
            pool.wait_ge(pool_step, 2)
            nc.gpsimd.affine_select(out=ident[:, :], in_=ident[:, :], compare_op=ALU.not_equal, fill=1.0, base=0,
                                    pattern=[[-1, P]], channel_multiplier=1).then_inc(consts_ready, 1)
            nc.gpsimd.affine_select(out=mask[:, :], in_=mask[:, :], compare_op=ALU.is_ge, fill=NEG, base=0,
                                    pattern=[[-1, P]], channel_multiplier=1).then_inc(consts_ready, 1)
            nc.gpsimd.iota(iota8[:, :, :], pattern=[[0, GT], [1, NE]], base=0, channel_multiplier=0,
                           allow_small_or_imprecise_dtypes=True).then_inc(consts_ready, 1)

            pool.wait_ge(in_bcast, 16)
            for b in range(G):
                tile = xacc[:, slices(b, GT), :]
                pool.wait_ge(in_x[b], 16)
                nc.gpsimd.tensor_tensor(tile, tile, bcast[:, 0:D].unsqueeze(1).to_broadcast([P, GT, D]), ALU.add
                                        ).then_inc(x_ready, 1)

            def split(hi, lo, raw, half, done):
                nc.gpsimd.tensor_copy(hi, raw).then_inc(half, 1)
                pool.wait_ge(half, done[1])
                nc.gpsimd.tensor_tensor(lo, raw, hi.bitcast(F32), ALU.subtract).then_inc(done[0], 1)

            steps_per_quad = len(PARTS) + 2 * EPQ

            def split_part(t, i, step):
                wait_apart(pool, in_raw[i], t * 16, (proj_qk, proj_v, proj_o)[i], t * (G * (4, 2, 2)[i]))
                part = PARTS[i]
                split(w_hi[:, part, :, :], w_lo[:, part, :, :], w_raw[:, part, :, :], pool_half,
                      (w_split[i], (t - 1) * steps_per_quad + step))

            with pool.Fori(1, QUADS) as t:
                split_part(t, 0, 1)
                split_part(t, 1, 2)
                for e3 in range(EPQ):
                    for i, (hi, lo) in enumerate(((up_hi, up_lo), (down_hi, down_lo))):
                        e = t * EPQ + (e3 - EPQ)
                        wait_apart(pool, in_ex[i], e * 16 + 16)
                        split(hi[:, bass.ds(e, 1), :].rearrange("p e n -> p (e n)"),
                              lo[:, bass.ds(e, 1), :].rearrange("p e n -> p (e n)"), ex_raw[:, i, :], pool_half,
                              (ex_split[i], (t - 1) * steps_per_quad + (2 * e3 + i + 3)))
                split_part(t, 2, steps_per_quad)

            def x2_lo(g):
                cols_g = bass.ds(g * GROUP, GROUP)
                for k in range(KT):
                    pool.wait_ge(x2_hi_ready, g * 2 + (k + 1))
                    pool.wait_ge(x2_t_ready, g * 2 + (k + 1))
                    nc.gpsimd.tensor_tensor(xt_lo[:, k, cols_g], x2_t[:, k, :], xt_hi[:, k, cols_g].bitcast(F32),
                                            ALU.subtract).then_inc(x2_split, 1)

            def hidden_lo(g, front):
                for e in range(NX):
                    for m in range(2 if e < NX - 1 else 1):
                        pool.wait_ge(hid_hi_done, g * (2 * NX) + (2 * e + m + 1))
                        nc.gpsimd.tensor_tensor(hid_lo[e % 2][:, m, :], hid[e % 2][:, m, :],
                                                hid_hi[e % 2][:, m, :].bitcast(F32), ALU.subtract).then_inc(hid_ready, 1)
                    if front and e == X2_TURN:
                        x2_lo(g + 1)

            roots = 2 + 4 * NEWTON
            done = 0

            def root_wait(ins):
                nonlocal done
                done += 1
                ins.then_inc(rstd_ready if done % roots == 0 else root_step, 1)
                if done % roots != 0:
                    pool.wait_ge(root_step, done - done // roots)

            pool.wait_ge(var_ready, 1)
            inverse_root(nc.gpsimd, FRONT, root_wait)
            pool.wait_ge(x1_ready, 1)
            nc.gpsimd.tensor_tensor(x1, x1, bcast[:, D:2 * D].unsqueeze(1).to_broadcast([P, GT, D]), ALU.add
                                    ).then_inc(bout_added, 1)
            pool.wait_ge(var_ready, 2)
            inverse_root(nc.gpsimd, FRONT, root_wait)
            x2_lo(0)
            hidden_lo(0, True)
            with pool.Fori(1, G - 1) as g:
                hidden_lo(g, True)
            hidden_lo(G - 1, False)

        @block.tensor
        def _(pe):
            def project_qk(part, pair, g, o):
                for k in range(KT):
                    mm = three(pe, o, w_hi[:, part, k, slices(pair, P)], w_lo[:, part, k, slices(pair, P)],
                               xt_hi[:, k, slices(g, GROUP)], xt_lo[:, k, slices(g, GROUP)], k == 0, k == KT - 1)
                mm.then_inc(proj_qk, 1)

            def project_v(half, g, o):
                for j in range(2):
                    tok = slices(g * GT + half * 2 + j, P)
                    for k in range(KT):
                        mm = three(pe, o[:, slices(j, QW)], xt_hi[:, k, tok], xt_lo[:, k, tok],
                                   w_hi[:, V, k, :], w_lo[:, V, k, :], k == 0, k == KT - 1)
                mm.then_inc(proj_v, 1)

            def project_o(half, o):
                for j in range(2):
                    tok = slices(half * 2 + j, P)
                    for k in range(KT):
                        mm = three(pe, o[:, slices(j, D)], ot_hi[:, k, tok], ot_lo[:, k, tok],
                                   w_hi[:, O, k, :], w_lo[:, O, k, :], k == 0, k == KT - 1)
                mm.then_inc(proj_o, 1)

            pe.wait_ge(consts_ready, 3)
            for _ in range(WARM_UP):
                pe.matmul(bank[0][:, 0:P], ident[:, :], ident[:, :], start=True, stop=True)
            pe.wait_ge(xt_ready, 1)
            pe.wait_ge(q_split, 1)
            for f in range(4):
                if f == 2:
                    pe.wait_ge(w_split[0], 1)
                if f >= 2:
                    pe.wait_ge(qk_ready, f - 1)
                project_qk((Q, K)[f // 2], f % 2, 0, pj_bank[f % 2][:, :])
            for f in range(2):
                pe.wait_ge(qk_ready, 3 + f)
                pe.wait_ge(w_split[1], 1)
                project_v(f, 0, pj_bank[f][:, :])

            def cross_weights(r):
                pe.wait_ge(in_cross, 16 * (r + 1))
                for i in range(2):
                    for m in range(KT):
                        mm = pe.matmul(bank[7][:, slices(m, D)], ex_raw[:, 0, i * D + m * P:i * D + (m + 1) * P],
                                       ex_raw[:, 1, slices(i, D)], start=(r == 0 and i == 0 and m == 0),
                                       stop=(r == G - 1 and i == 1), skip_group_check=True)
                mm.then_inc(wvo_step, 1)

            def slot(s):
                def fill(f):
                    o = (pj_bank if s.proj else s.o_bank)[f % 2][:, :]
                    if s.pp == 0 and s.proj:
                        if f < 2:
                            pe.wait_ge(v_ready, s.u(2, f + 1))
                            if s.static is None or s.static >= 4:
                                pe.wait_ge(o_added, s.u(2, f - 3))
                        else:
                            pe.wait_ge(qk_ready, s.u(4, 4 + f - 1))
                        if f == 0 and s.static is not None and s.gn > 0:
                            pe.wait_ge(xt_ready, s.gn + 1)
                        if f == 0 and s.gn == 0:
                            pe.wait_ge(w_split[0], s.qn + 1)
                        project_qk((Q, K)[f // 2], f % 2, s.gn, o)
                    if s.pp == 1 and f < 2 and s.proj:
                        pe.wait_ge(qk_ready, s.u(4, 4 + 3 + f))
                        if f == 0 and s.gn == 0:
                            pe.wait_ge(w_split[1], s.qn + 1)
                        project_v(f, s.gn, o)
                    if s.oproj and f >= 2:
                        if s.proj:
                            pe.wait_ge(v_ready, s.u(2, 2 + f - 1))
                        elif (s.static, f) in ((SLOTS - 1, 3), (SLOTS + 1, 2)):
                            pe.wait_ge(o_added, s.u(2, f - 4))
                        elif s.static != SLOTS + 1:
                            pe.wait_ge(o_added, s.u(2, f - 1 - 4))
                        if f == 2:
                            pe.wait_ge(ot_ready, s.u(2, 0))
                            if s.go == 0:
                                pe.wait_ge(w_split[2], s.qo + 1)
                        project_o(f - 2, o)

                def score():
                    pe.wait_ge(qk_ready, s.u(4, 4))
                    if s.first > 0 or s.static is None:
                        pe.wait_ge(masked, s.n(8, 0))
                    for j in range(GT):
                        for h in range(2):
                            rows_h = slices(h, DH)
                            mm = pe.matmul(sc_bank[h][:, slices(j, P)], qt[s.ub][rows_h, s.pp, slices(j, P)],
                                           kt[s.ub][rows_h, s.pp, slices(j, P)], start=True, stop=True)
                            if j == GT - 1:
                                mm.then_inc(scores, 1)

                def turn(h):
                    pe.wait_ge(probs_ready, s.n(2, h - 1))
                    if s.static is None or s.static >= 2:
                        pe.wait_ge((pt_a, pt_b)[h], s.n(1, -1))
                    for j in range(GT):
                        mm = pe.transpose(tr_bank[h][:, slices(j, P)], probs[:, 1 - s.par, h, slices(j, P)], ident[:, :])
                    mm.then_inc(transposed, 1)

                if s.front:
                    score()
                if s.back:
                    turn(0)
                fill(0)
                if s.back:
                    turn(1)
                fill(1)
                if s.static == SLOTS - 1:
                    x2_turn(0)
                fill(2)
                if s.static == SLOTS:
                    route(0)
                    up(0, 0)
                if s.back:
                    pe.wait_ge(pt_a, s.n(1, 0))
                    pe.wait_ge(pt_b, s.n(1, 0))
                    pe.wait_ge(v_ready, s.u(2, 2 if s.pp == 1 else 0))
                    if s.static is None or s.static >= 2:
                        pe.wait_ge(ot_ready, s.n(1, -1))
                    vb = vv[s.ub if s.pp == 1 else 1 - s.ub]
                    for j in range(GT):
                        for h in range(2):
                            c = (1 - s.pp) * P + h * DH
                            mm = pe.matmul(pv_bank[slices(h, DH), slices(j, P)], vb[:, j, c:c + DH],
                                           probs_t[:, h, slices(j, P)], start=True, stop=True)
                    mm.then_inc(pv_done, 1)
                fill(3)

            def cross(g, half):
                if half == 0:
                    pe.wait_ge(in_ctx, g * 16 + 16)
                    pe.wait_ge(wvo_ready, 1)
                if isinstance(g, int) and g == 0:
                    o = fr_bank[1]
                    if half == 1:
                        pe.wait_ge(cross_used, 1)
                else:
                    o = fr_bank[half]
                    pe.wait_ge(bias_used, g * 2)
                for j in range(2):
                    for k in range(KT):
                        mm = pe.matmul(o[:, slices(j, D)], ctx_t[:, k, slices(2 * half + j, P)], wvo[:, k, :],
                                       start=(k == 0), stop=(k == KT - 1))
                mm.then_inc(cross_done, 1)

            def x2_turn(g):
                pe.wait_ge(x2_ready, g + 1)
                if isinstance(g, int) and g == 0:
                    pe.wait_ge(o_added, 2 * UNITS - 4)
                for k in range(KT):
                    for j in range(GT):
                        mm = pe.transpose(fr_bank[k][:, slices(j, P)], x2[:, j, slices(k, P)], ident[:, :])
                mm.then_inc(x2_tp, 1)

            def route(g):
                pe.wait_ge(x2_t_ready, g * 2 + 2)
                pe.wait_ge(x2_hi_ready, g * 2 + 2)
                for j in range(GT):
                    for k in range(KT):
                        mm = pe.matmul(fr_bank[0][:, slices(j, NE)], x2_t[:, k, slices(j, P)], gate[:, k, :],
                                       start=(k == 0), stop=(k == KT - 1))
                mm.then_inc(logit_done, 1)

            def comb_turn(g):
                pe.wait_ge(comb_ready, g + 1)
                for j in range(GT):
                    mm = pe.transpose(fr_bank[1][0:NX, slices(j, P)], comb[:, j, :], ident[:, :])
                mm.then_inc(comb_tp, 1)

            def bias(g):
                pe.wait_ge(comb_t_ready, g + 1)
                for j in range(GT):
                    mm = pe.matmul(fr_bank[j // 2][:, slices(j % 2, D)], comb_t[:, slices(j, P)], down_b[:, :],
                                   start=True, stop=True)
                    if j % 2 == 1:
                        mm.then_inc(bias_done, 1)

            def up(g, e):
                if e == 0:
                    pe.wait_ge(x2_split, g * 2 + 2)
                if isinstance(g, int) and g == 0 and e < 2:
                    if e == 0:
                        pe.wait_ge(masked, 8 * SLOTS)
                        pe.wait_ge(ex_split[0], NX)
                        pe.wait_ge(ex_split[1], NX)
                    else:
                        pe.wait_ge(pt_a, SLOTS)
                        pe.wait_ge(pt_b, SLOTS)
                else:
                    before = {0: 0, 1: -1}.get(e, e - 1)
                    pe.wait_ge(silu_done, g * (2 * NX) + 2 * before)
                for m in range(2):
                    for k in range(KT):
                        c = slice(k * D + m * P, k * D + (m + 1) * P)
                        cols_g = bass.ds(g * GROUP, GROUP)
                        mm = three(pe, up_bank[e % 2][m][:, :], up_hi[:, e, c], up_lo[:, e, c],
                                   xt_hi[:, k, cols_g], xt_lo[:, k, cols_g], k == 0, k == KT - 1)
                    mm.then_inc(up_done, 1)

            def down(g, e):
                pe.wait_ge(hid_ready, g * HALVES + min(2 * e + 2, HALVES))
                if e == NX - 1:
                    pe.wait_ge(hid_last_ready, g + 1)
                for half in range(2):
                    if isinstance(g, int) and g == 0 and e == 0:
                        pe.wait_ge(o_added, 2 * UNITS)
                    else:
                        pe.wait_ge(down_used, g * (2 * NX) + (2 * e - 1 + half))
                    for j in (2 * half, 2 * half + 1):
                        for k in range(KT):
                            mm = three(pe, dn_bank[half][:, slices(j % 2, D)], hid_hi[e % 2][:, k, slices(j, P)],
                                       hid_lo[e % 2][:, k, slices(j, P)], down_hi[:, e, slices(k, D)],
                                       down_lo[:, e, slices(k, D)], k == 0, k == KT - 1)
                    mm.then_inc(down_done, 1)

            def ffn_and_front(g, front, started=0):
                for e in range(NX + LAG):
                    if started <= e < NX:
                        up(g, e)
                    if e == 1:
                        comb_turn(g)
                    if e == 2:
                        bias(g)
                    if e >= LAG:
                        down(g, e - LAG)
                    if front and e == CROSS:
                        cross(g + 1, 0)
                        cross(g + 1, 1)
                    if front and e == X2_TURN:
                        x2_turn(g + 1)
                    if front and e == ROUTE:
                        route(g + 1)

            pe.wait_ge(in_small, 32)
            cross_weights(0)
            all_slots(pe, slot, {0: lambda: cross_weights(1), 1: lambda: cross_weights(2),
                                 2: lambda: cross_weights(3),
                                 27: lambda: cross(0, 0), 29: lambda: cross(0, 1),
                                 32: lambda: up(0, 1)})
            ffn_and_front(0, True, started=2)
            with pe.Fori(1, G - 1) as g:
                ffn_and_front(g, True)
            ffn_and_front(G - 1, False)

        @block.scalar
        def _(act):
            act.wait_ge(table_ready, 1)
            nc.scalar.activation(root_sq[:, 0, :], root_sq[:, 0, :], ACT.Exp)
            act.dma_start(cols[:, :], col_bias).then_inc(in_cols, 16)
            act.dma_start(down_b[:, :], down_bias).then_inc(in_small, 16)
            act.dma_start(gate[:, :, :], w_gate).then_inc(in_small, 16)

            def split_xt(b):
                act.wait_ge(in_xt[b], 16)
                nc.scalar.activation(xt_hi[:, :, slices(b, GROUP)], xt_raw[b], ACT.Copy).then_inc(xt_hi_ready, 1)

            for k in range(KT):
                act.wait_ge(in_xt0[k], 16)
                nc.scalar.activation(xt_hi[:, k, 0:GROUP], xt_raw[0][:, k, :], ACT.Copy).then_inc(xt_hi_ready, 1)
            act.dma_start(bcast[:, :], row_bias.partition_broadcast(P)).then_inc(in_bcast, 16)

            def take_qk(f, g, quad, ub):
                dst = (qt, kt)[f // 2][ub][:, f % 2, :]
                b = cols[:, bass.ds(quad * 2 + ((f // 2) * IT + f % 2), 1)]
                nc.scalar.activation(dst, pj_bank[f % 2][:, :], ACT.Identity, bias=b).then_inc(qk_ready, 1)

            def take_wvo():
                act.wait_ge(wvo_step, G)
                nc.scalar.activation(wvo[:, :, :], bank[7][:, :].rearrange("p (k n) -> p k n", k=KT), ACT.Copy
                                     ).then_inc(wvo_ready, 1)

            def take_v(f, ub):
                nc.scalar.activation(vv[ub][:, 2 * f:2 * f + 2, :],
                                     pj_bank[f][:, :].rearrange("p (j n) -> p j n", j=2), ACT.Copy).then_inc(v_ready, 1)

            act.wait_ge(in_cols, 16)
            for f in range(4):
                act.wait_ge(proj_qk, f + 1)
                take_qk(f, 0, 0, 0)
                if f == 1:
                    split_xt(1)
            for f in range(2):
                act.wait_ge(proj_v, f + 1)
                take_v(f, 0)
            for b in range(2, G):
                split_xt(b)

            def slot(s):
                def take(f):
                    if s.pp == 0 and s.proj:
                        wait_apart(act, proj_qk, s.u(4, 4 + f + 1))
                        take_qk(f, s.gn, s.qn, 1 - s.ub)
                    if s.pp == 1 and f < 2 and s.proj:
                        act.wait_ge(proj_v, s.u(2, 2 + f + 1))
                        take_v(f, 1 - s.ub)

                def exps(h):
                    for j in range(GT):
                        act.wait_ge(masked, s.n(8, 4 * h + j + 1))
                        tile = probs[:, s.par, h, slices(j, P)]
                        nc.scalar.activation(tile, tile, ACT.Exp, scale=-1.0, bias=negmax[:, s.par, h, j:j + 1],
                                             accum_out=sums[:, s.par, h, j:j + 1]).then_inc(exped, 1)

                def take_pt_b():
                    act.wait_ge(transposed, s.n(2, 0))
                    nc.scalar.activation(probs_t[:, 1, :], tr_bank[1][:, :], ACT.Copy).then_inc(pt_b, 1)

                if s.evac_o:
                    waits = (pv_done, s.n(1, -1))
                    if s.pp == 0 and (s.static is None or s.static >= 4):
                        waits += (proj_o, s.u(2, -2))
                    wait_apart(act, *waits)
                    nc.scalar.activation(ot_hi[:, s.pp, :], pv_bank[:, :], ACT.Identity, bias=v_bias(s)
                                         ).then_inc(ot_hi_ready, 1)
                if s.act_turns:
                    act.wait_ge(transposed, s.n(2, -1))
                    nc.scalar.activation(probs_t[:, 0, :], tr_bank[0][:, :], ACT.Copy).then_inc(pt_a, 1)
                    take_pt_b()
                if s.front:
                    exps(0)
                take(0)
                if s.back and not s.act_turns:
                    take_pt_b()
                if s.static == 0:
                    take(1)
                    exps(1)
                else:
                    if s.front:
                        exps(1)
                    take(1)
                take(2)
                take(3)

            def take_x2(g):
                act.wait_ge(x2_tp, g + 1)
                for k in range(KT):
                    nc.scalar.activation(xt_hi[:, k, bass.ds(g * GROUP, GROUP)], fr_bank[k][:, :], ACT.Copy
                                         ).then_inc(x2_hi_ready, 1)
                    nc.scalar.activation(x2_t[:, k, :], fr_bank[k][:, :], ACT.Copy).then_inc(x2_t_ready, 1)

            def route_exp(g):
                act.wait_ge(shift_ready, g + 1)
                nc.scalar.activation(expd[:, :, :], shifted[:, :, :], ACT.Exp).then_inc(exp_ready, 1)

            def take_comb(g):
                act.wait_ge(comb_tp, g + 1)
                nc.scalar.activation(comb_t[:, :], fr_bank[1][0:NX, :], ACT.Copy).then_inc(comb_t_ready, 1)

            def hidden(g, e):
                fresh = isinstance(g, int) and g == 0 and e < 2
                before = {0: 0, 1: -1}.get(e, e - 1)
                if not fresh:
                    act.wait_ge(hid_ready, g * HALVES + (2 * before if before >= 0 else -1))
                    if e == 0:
                        act.wait_ge(hid_last_ready, g)
                for m in range(2):
                    act.wait_ge(up_done, g * (2 * NX) + (2 * e + m + 1))
                    b = 3 * IT + 2 * e + m
                    nc.scalar.activation(hid[e % 2][:, m, :], up_bank[e % 2][m][:, :], ACT.Silu,
                                         bias=cols[:, b:b + 1]).then_inc(silu_done, 1)
                if not fresh:
                    act.wait_ge(down_done, g * (2 * NX) + 2 * before)
                elif e == 1:
                    act.wait_ge(proj_o, 2 * UNITS)
                for m in range(2):
                    act.wait_ge(silu_done, g * (2 * NX) + (2 * e + m + 1))
                    nc.scalar.activation(hid_hi[e % 2][:, m, :], hid[e % 2][:, m, :], ACT.Copy).then_inc(hid_hi_done, 1)

            def ffn_and_front(g, front, started=0):
                for e in range(started, NX):
                    hidden(g, e)
                    if e == 1:
                        take_comb(g)
                    if front and e == X2_TURN:
                        take_x2(g + 1)
                    if front and e == ROUTE:
                        route_exp(g + 1)

            all_slots(act, slot, {2: take_wvo, 31: lambda: take_x2(0),
                                  32: lambda: (route_exp(0), hidden(0, 0))})
            ffn_and_front(0, True, started=1)
            with act.Fori(1, G - 1) as g:
                ffn_and_front(g, True)
            ffn_and_front(G - 1, False)

        @block.vector
        def _(dve):
            nc.vector.memset(root_sq[:, :, :], 0.0).then_inc(table_ready, 1)
            nc.vector.memset(rstd[:, :, :], 0.0).then_inc(out_done, 16)
            nc.vector.memset(comb[:, :, :], 1.0).then_inc(dve_step, 1)

            def xt_low(b, k, count):
                dve.wait_ge(xt_hi_ready, count)
                hi = xt_hi[:, k, slices(b, GROUP)]
                return nc.vector.tensor_tensor(xt_lo[:, k, slices(b, GROUP)], xt_raw[b][:, k, :], hi.bitcast(F32),
                                               ALU.subtract)

            def split_xt(b):
                xt_low(b, slice(0, KT), KT + b).then_inc(xt_ready, 1)

            def split_part(part, done):
                dve.wait_ge(in_quad[part], 16)
                nc.vector.tensor_copy(w_hi[:, part, :, :], w_raw[:, part, :, :]).then_inc(dve_step, 1)
                dve.wait_ge(dve_step, 2 + part)
                nc.vector.tensor_tensor(w_lo[:, part, :, :], w_raw[:, part, :, :], w_hi[:, part, :, :].bitcast(F32),
                                        ALU.subtract).then_inc(done, 1)

            split_part(Q, q_split)
            xt_low(0, 0, 1)
            xt_low(0, 1, 2).then_inc(xt_ready, 1)
            split_part(K, w_split[0])
            split_part(V, w_split[1])
            split_xt(1)
            split_part(O, w_split[2])
            dve.wait_ge(consts_ready, 3)

            def slot(s, early={}, inside={}):
                def mask_and_max(h):
                    wait_apart(dve, scores, s.n(2, h + 1))
                    for j in range(GT):
                        nc.vector.tensor_tensor_reduce(
                            probs[:, s.par, h, slices(j, P)], sc_bank[h][:, slices(j, P)], mask[:, :], -SCALE, 3.0e38,
                            ALU.add, ALU.min, negmax[:, s.par, h, j:j + 1]).then_inc(masked, 1)

                def normalise(h):
                    dve.wait_ge(exped, s.n(8, 4 * h + 4))
                    nc.vector.reciprocal(rsum[:, h, :], sums[:, s.par, h, :]).then_inc(rsum_ready, 1)
                    dve.wait_ge(rsum_ready, s.n(2, h + 1))
                    tile = probs[:, s.par, h, :].rearrange("p (j k) -> p j k", j=GT)
                    nc.vector.tensor_tensor(tile, tile, rsum[:, h, :].unsqueeze(2).to_broadcast([P, GT, P]), ALU.mult
                                            ).then_inc(probs_ready, 1)

                def add_o(half):
                    dve.wait_ge(proj_o, s.u(2, half - 1))
                    if half == 0 and s.static is None:
                        dve.wait_ge(x_ready, s.go + 1)
                    o = s.o_bank[half]
                    tile = xacc[:, s.go * GT + 2 * half:s.go * GT + 2 * half + 2, :]
                    nc.vector.tensor_tensor(tile, o[:, :].rearrange("p (j n) -> p j n", j=2), tile,
                                            ALU.add).then_inc(o_added, 1)

                if s.evac_o:
                    dve.wait_ge(ot_hi_ready, s.n(1, -1))
                    nc.vector.scalar_tensor_tensor(out=ot_lo[:, s.pp, :], in0=pv_bank[:, :], scalar=v_bias(s),
                                                   in1=ot_hi[:, s.pp, :].bitcast(F32), op0=ALU.add,
                                                   op1=ALU.subtract).then_inc(ot_ready, 1)
                if s.front:
                    mask_and_max(0)
                early.get(s.static, lambda: None)()
                if s.front:
                    mask_and_max(1)
                if s.back and not s.act_turns:
                    dve.wait_ge(transposed, s.n(2, -1))
                    nc.vector.tensor_copy(probs_t[:, 0, :], tr_bank[0][:, :]).then_inc(pt_a, 1)
                if s.front:
                    normalise(0)
                inside.get(s.static, lambda: None)()
                if s.oproj:
                    add_o(0)
                if s.front:
                    normalise(1)
                if s.oproj:
                    add_o(1)

            class Chain:
                per_body = BODY_STEPS
                c, g = 1 + (O + 1), 0

                def step(s, ins, wait=lambda eng, semaphore, value: eng.wait_ge(semaphore, value)):
                    s.c += 1
                    ins.then_inc(dve_step, 1)
                    wait(dve, dve_step, s.g * s.per_body + s.c)

            ch = Chain()

            def moments(sources):
                for which, src in sources:
                    for j in range(GT):
                        last = nc.vector.bn_stats(stats[:, which, j, :], src(j))
                ch.step(last, wait_apart)
                for which, src in sources:
                    for j in range(GT):
                        last = nc.vector.bn_aggr(mv[:, which, j, :], stats[:, which, j, :])
                return last

            def statistics(sources):
                ch.step(moments(sources), wait_apart)
                inverse_root(nc.vector, slice(sources[0][0], sources[-1][0] + 1), ch.step)

            def apply(src, dst, which, tiles=range(GT)):
                for j in tiles:
                    last = nc.vector.tensor_scalar(dst[:, j, :], src(j), mv[:, which, j, 0:1],
                                                   rstd[:, which, j:j + 1], ALU.subtract, ALU.mult)
                return last

            def tile_of(g):
                def src(j):
                    return xacc[:, bass.ds(g * GT + j, 1), :].rearrange("p t n -> p (t n)")
                return src

            def of_y(j):
                return yacc[:, j, :]

            def of_x1(j):
                return x1[:, j, :]

            def open_stats(g, front):
                sources = [(0, tile_of(g + 1))] if front else []
                first = isinstance(g, int) and g == 0
                if not first:
                    dve.wait_ge(down_used, g * (2 * NX))
                    sources.append((1, of_y))
                statistics(sources)
                if not first:
                    dve.wait_ge(out_done, g * 16)
                    apply(of_y, yout, 1).then_inc(y_ready, 1)

            def norm1(g):
                return apply(tile_of(g), x1, 0)

            def add_bout():
                ch.step(nc.vector.tensor_tensor(x1, x1, bcast[:, D:2 * D].unsqueeze(1).to_broadcast([P, GT, D]),
                                                ALU.add))

            def add_cross(g, half):
                dve.wait_ge(cross_done, g * 2 + (half + 1))
                tile = x1[:, 2 * half:2 * half + 2, :]
                o = fr_bank[1 if isinstance(g, int) and g == 0 else half]
                nc.vector.tensor_tensor(tile, o[:, :].rearrange("p (j n) -> p j n", j=2), tile, ALU.add
                                        ).then_inc(cross_used, 1)

            def norm2_stats(g):
                dve.wait_ge(cross_used, g * 2 + 2)
                if isinstance(g, int) and g == 0:
                    moments([(0, of_x1)]).then_inc(var_ready, 1)
                else:
                    statistics([(0, of_x1)])

            def norm2(g):
                apply(of_x1, x2, 0).then_inc(x2_ready, 1)

            def best_two(g):
                dve.wait_ge(logit_done, g + 1)
                ch.step(nc.vector.tensor_copy(logits[:, :, :],
                                              fr_bank[0][:, 0:GT * NE].rearrange("p (j e) -> p j e", j=GT)),
                        wait_apart)
                for j in range(GT):
                    last = nc.vector.max(top8[:, j, :], logits[:, j, :])
                ch.step(last)
                top = top8[:, :, 0:1]
                nc.vector.tensor_tensor(shifted[:, :, 0:NE], logits[:, :, :], top.to_broadcast([P, GT, NE]), ALU.subtract)
                nc.vector.tensor_tensor(shifted[:, :, NE:NE + 2], top8[:, :, 0:2], top.to_broadcast([P, GT, 2]),
                                        ALU.subtract).then_inc(shift_ready, 1)
                for j in range(GT):
                    last = nc.vector.max_index(idx8[:, j, :], top8[:, j, :], logits[:, j, :])
                ch.step(last)
                ch.step(nc.vector.tensor_copy(idx2[:, :, :], idx8[:, :, 0:2]))
                for i in range(2):
                    last = nc.vector.tensor_tensor(hot[:, i, :, :], iota8[:, :, :],
                                                   idx2[:, :, i:i + 1].to_broadcast([P, GT, NE]), ALU.is_equal)
                ch.step(last)

            def weigh(g):
                dve.wait_ge(exp_ready, g + 1)
                ch.step(nc.vector.tensor_reduce(zsum[:, :], expd[:, :, 0:NE], AX.X, ALU.add))
                ch.step(nc.vector.reciprocal(rz[:, :], zsum[:, :]))
                ch.step(nc.vector.tensor_tensor(best[:, :, :], expd[:, :, NE:NE + 2],
                                                rz[:, :].unsqueeze(2).to_broadcast([P, GT, 2]), ALU.mult))
                ch.step(nc.vector.tensor_reduce(bsum[:, :], best[:, :, :], AX.X, ALU.add))
                ch.step(nc.vector.tensor_scalar(bsum[:, :], bsum[:, :], 1e-20, None, ALU.add))
                ch.step(nc.vector.reciprocal(rb[:, :], bsum[:, :]))
                ch.step(nc.vector.tensor_tensor(wbest[:, :, :], best[:, :, :],
                                                rb[:, :].unsqueeze(2).to_broadcast([P, GT, 2]), ALU.mult))
                for i in range(2):
                    last = nc.vector.tensor_tensor(hot[:, i, :, :], hot[:, i, :, :],
                                                   wbest[:, :, i:i + 1].to_broadcast([P, GT, NE]), ALU.mult)
                ch.step(last)
                nc.vector.tensor_tensor(comb[:, :, 0:NE], hot[:, 0, :, :], hot[:, 1, :, :], ALU.add
                                        ).then_inc(comb_ready, 1)

            def start_y(g):
                dve.wait_ge(comb_ready, g + 1)
                nc.vector.tensor_copy(comb_f[:, :, :], comb[:, :, :])
                if not (isinstance(g, int) and g == 0):
                    dve.wait_ge(y_ready, g)
                for half in range(2):
                    dve.wait_ge(bias_done, g * 2 + (half + 1))
                    nc.vector.tensor_tensor(yacc[:, 2 * half:2 * half + 2, :],
                                            fr_bank[half][:, :].rearrange("p (j n) -> p j n", j=2),
                                            x2[:, 2 * half:2 * half + 2, :], ALU.add).then_inc(bias_used, 1)
                dve.wait_ge(bias_used, g * 2 + 2)

            def add_expert(g, e, behind=lambda tiles: None):
                for half in range(2):
                    dve.wait_ge(down_done, g * (2 * NX) + (2 * e + half + 1))
                    if e > 0:
                        dve.wait_ge(down_used, g * (2 * NX) + (2 * e - 1 + half))
                    tiles = (2 * half, 2 * half + 1)
                    for j in tiles:
                        last = nc.vector.scalar_tensor_tensor(
                            out=yacc[:, j, :], in0=dn_bank[half][:, slices(j % 2, D)], scalar=comb_f[:, j, e:e + 1],
                            in1=yacc[:, j, :], op0=ALU.mult, op1=ALU.add)
                    last.then_inc(down_used, 1)
                    behind(tiles)

            def last_lo(g):
                e = NX - 1
                dve.wait_ge(hid_hi_done, (g + 1) * (2 * NX))
                nc.vector.tensor_tensor(hid_lo[e % 2][:, 1, :], hid[e % 2][:, 1, :],
                                        hid_hi[e % 2][:, 1, :].bitcast(F32), ALU.subtract).then_inc(hid_last_ready, 1)

            def finish():
                g = G - 1

                def stats_of(tiles):
                    dve.wait_ge(down_used, G * (2 * NX) - 1 + tiles[0] // 2)
                    for j in tiles:
                        last = nc.vector.bn_stats(stats[:, 1, j, :], of_y(j))
                    ch.step(last)

                add_expert(g, NX - 1, stats_of)
                for j in range(GT):
                    last = nc.vector.bn_aggr(mv[:, 1, j, :], stats[:, 1, j, :])
                ch.step(last)
                inverse_root(nc.vector, LAST, ch.step)
                dve.wait_ge(out_done, G * 16)
                for half in range(2):
                    apply(of_y, yout, 1, (2 * half, 2 * half + 1)).then_inc(y_ready, 1)

            def ffn_and_front(g, front):
                ch.g, ch.c = g, FRONT_STEPS
                open_stats(g, front)
                start_y(g)
                for e in range(NX if front else NX - 1):
                    add_expert(g, e)
                    if e == NX - 3:
                        last_lo(g)
                    if front and e == 0:
                        ch.step(norm1(g + 1))
                        add_bout()
                    if front and e + LAG == CROSS:
                        add_cross(g + 1, 0)
                        add_cross(g + 1, 1)
                        norm2_stats(g + 1)
                    if front and e + LAG == CROSS + 1:
                        norm2(g + 1)
                    if front and e + LAG == ROUTE:
                        best_two(g + 1)
                    if front and e + LAG == ROUTE + 1:
                        weigh(g + 1)
                if front:
                    ch.c - FRONT_STEPS == BODY_STEPS or fail(ch.c - FRONT_STEPS)
                else:
                    finish()

            def fail(n):
                raise ValueError(f"{n} steps of VectorE per group")

            def norm1_stats0():
                dve.wait_ge(o_added, 2 * (UNITS - G + 1))
                moments([(0, tile_of(0))]).then_inc(var_ready, 1)

            def norm1_0():
                dve.wait_ge(rstd_ready, 1)
                norm1(0).then_inc(x1_ready, 1)

            def add_cross0():
                dve.wait_ge(bout_added, 1)
                add_cross(0, 0)

            def norm2_0():
                dve.wait_ge(rstd_ready, 2)
                norm2(0)

            early = {30: lambda: (add_cross(0, 1), norm2_stats(0))}
            inside = {28: norm1_0, 29: add_cross0}
            all_slots(dve, lambda s: slot(s, early, inside),
                      {0: lambda: split_xt(2), 1: lambda: split_xt(3), 27: norm1_stats0, 30: norm2_0,
                       32: lambda: (best_two(0), weigh(0))})
            dve.wait_ge(o_added, 2 * UNITS)
            ch.c == FRONT_STEPS or fail(ch.c)
            ffn_and_front(0, True)
            with dve.Fori(1, G - 1) as g:
                ffn_and_front(g, True)
            ffn_and_front(G - 1, False)


def kernel(**inputs):
    import numpy as np
    import concourse.bacc as bacc
    from concourse.bass_utils import run_bass_kernel_spmd

    a = {k: np.asarray(v) for k, v in inputs.items()}

    def heads_in(w):
        return w.reshape(QUADS, 4, KT, P, DH).transpose(0, 3, 2, 1, 4).reshape(QUADS, P, KT, QW)

    w_o = a["L0_attn_O_w"].reshape(INNER, D)
    o_quads = w_o.reshape(QUADS, KT, P, D).transpose(0, 2, 1, 3)
    w_v_t = a["L0_xattn_Wkv"][:, INNER:].T
    w_out = a["L0_xattn_Wout"]
    up = np.concatenate([a["L0_ffn_up_w"], a["L0_ffn_sh_up_w"][None]])
    down = np.concatenate([a["L0_ffn_down_w"], a["L0_ffn_sh_down_w"][None]])
    up_b = np.concatenate([a["L0_ffn_up_b"], a["L0_ffn_sh_up_b"][None]])

    def by_partition(w):
        return w.reshape(NX, KT, P, D).transpose(0, 2, 1, 3).reshape(NX, P, KT * D)

    arrays = {
        "x": a["x"].reshape(TOK, D),
        "x_t": a["x"].reshape(TOK, D).T,
        "ctx_t_in": a["ctx_1024"].reshape(TOK, D).T,
        "w_quads": np.stack([heads_in(a["L0_attn_Q_w"]), heads_in(a["L0_attn_K_w"]), heads_in(a["L0_attn_V_w"]),
                             o_quads], axis=2),
        "w_cross": np.concatenate([w_v_t.reshape(4, 1, 2, P, D), w_out.reshape(4, 1, 2, P, D)], axis=1
                                  ).transpose(0, 3, 1, 2, 4).reshape(4, P, 2, 2 * D),
        "w_experts": np.stack([by_partition(up), by_partition(down)]),
        "w_gate": a["L0_ffn_gate_w"].T.reshape(KT, P, NE).transpose(1, 0, 2),
        "col_bias": np.concatenate([a[f"L0_attn_{n}_b"].reshape(IT, P).T for n in "QKV"]
                                   + [up_b.reshape(2 * NX, P).T], axis=1),
        "row_bias": np.concatenate([a["L0_attn_O_b"], a["L0_xattn_bout"]]),
        "down_bias": np.concatenate([a["L0_ffn_down_b"], a["L0_ffn_sh_down_b"][None]]),
    }
    arrays = {k: np.ascontiguousarray(v) for k, v in arrays.items()}
    nc = bacc.Bacc("TRN2", target_bir_lowering=False, num_devices=1)
    aps = {k: nc.dram_tensor(f"in_{k}", v.shape, F32, kind="ExternalInput").ap() for k, v in arrays.items()}
    out = nc.dram_tensor("out_0", (TOK, D), F32, kind="ExternalOutput").ap()
    decoder_program(nc, out=out, **aps)
    r = run_bass_kernel_spmd(nc, [{f"in_{k}": v for k, v in arrays.items()}], core_ids=[0])
    return r.results[0]["out_0"].reshape(SEQS, S, D)
```
